# Optimizing a Trainium2 kernel written in Bass

```python
import numpy as np
import jax
import jax.numpy as jnp

def _softmax(x, axis=-1):
    return jax.nn.softmax(x, axis=axis)

def _gelu(x):
    return jax.nn.gelu(x, approximate=True)

def _silu(x):
    return jax.nn.silu(x)

def _sigmoid(x):
    return jax.nn.sigmoid(x)

def _layernorm(x, axis=-1, eps=1e-05):
    m = jnp.mean(x, axis=axis, keepdims=True)
    v = jnp.var(x, axis=axis, keepdims=True)
    return (x - m) / jnp.sqrt(v + eps)

def _scatter_add(tgt, idx, src, axis=0):
    return tgt.at[idx].add(src)

def _segment_sum(src, seg, n):
    return jax.ops.segment_sum(src, seg, n)
kernel_name = 'mk_adj_resnorm_d4_adj_r2_531361'

def setup_inputs(seed: int=0):
    np.random.seed(seed)
    _w = jnp.asarray

    def _rec_inputs():
        import jax
        import jax.numpy as jnp
        _gk = jax.random.key(seed)
        x = -0.000929 + 1 * jax.random.normal(jax.random.fold_in(_gk, 1), (8, 2048, 64), jnp.float32)
        _a = jax.random.bernoulli(jax.random.fold_in(_gk, 2), 0.000976562, (8, 2048, 2048))
        _a = jnp.logical_or(_a, jnp.eye(2048, dtype=bool))
        _af = _a.astype(jnp.float32)
        _af = _af * jax.random.uniform(jax.random.fold_in(_gk, 3), (8, 2048, 2048), jnp.float32, 0.05, 1)
        adj = _af
        _nm = jnp.ones((8, 2048), dtype=bool)
        nodemask = jnp.where(_nm, 1.0, 0.0).astype(jnp.float32)
        return (x, adj, nodemask)
    x, adj, nodemask = _rec_inputs()

    def _L0_gnn_setup():
        import jax, jax.numpy as jnp
        import numpy as np
        B, N, C, R = (4, 2048, 64, 16)
        EPS = 1e-12
        key = jax.random.key(seed)
        k_x, k_w, k_u = jax.random.split(key, 3)
        x = jax.random.normal(k_x, (B, N, C), dtype=jnp.float32)
        W = jax.random.uniform(k_w, (B, N, N), dtype=jnp.float32)
        U = 0.01 * jax.random.normal(k_u, (N, R), dtype=jnp.float32)
        w_scale = jnp.asarray(1.0, dtype=jnp.float32)
        return {'x': x, 'W': W, 'U': U, 'w_scale': w_scale}
    _L0_gnn_all = _L0_gnn_setup()
    _L0_gnn_in = {k: v for k, v in _L0_gnn_all.items() if k in ('U', 'w_scale')}
    del _L0_gnn_all

    def _L1_gnn_setup():
        import jax, jax.numpy as jnp
        import numpy as np
        NORM = 1.0

        def _glorot(key, shape):
            fan_in, fan_out = shape
            lim = float(np.sqrt(6.0 / (fan_in + fan_out)))
            return jax.random.uniform(key, shape, jnp.float32, -lim, lim)

        def _gcn_layer(h, adj, W, b):
            msg = h @ W + b
            agg = jnp.einsum('bij,bjd->bid', adj, msg) / NORM
            return jax.nn.relu(agg)
        key = jax.random.key(seed)
        ks = jax.random.split(key, 12)
        B, N = (8, 1024)
        latent, hidden, out_dim = (64, 128, 64)
        inp = {'latent_features': jax.random.normal(ks[0], (B, N, latent), jnp.float32), 'adjacency_matrix': jax.random.uniform(ks[1], (B, N, N), jnp.float32), 'node_mask': jnp.ones((B, N, 1), jnp.float32), 'W0': _glorot(ks[2], (latent, hidden)), 'b0': jnp.zeros((hidden,), jnp.float32), 'W1': _glorot(ks[3], (hidden, hidden)), 'b1': jnp.zeros((hidden,), jnp.float32), 'W2': _glorot(ks[4], (hidden, hidden)), 'b2': jnp.zeros((hidden,), jnp.float32), 'Wout': _glorot(ks[5], (hidden, out_dim)), 'bout': jnp.zeros((out_dim,), jnp.float32)}
        return inp
    _L1_gnn_all = _L1_gnn_setup()
    _L1_gnn_in = {k: v for k, v in _L1_gnn_all.items() if k in ('W0', 'b0', 'W1', 'b1', 'W2', 'b2', 'Wout', 'bout')}
    del _L1_gnn_all

    def _L2_gnn_setup():
        import jax, jax.numpy as jnp
        import numpy as np
        B, N, F_IN, F_OUT = (128, 256, 64, 64)
        key = jax.random.key(seed)
        k1, k2, k3, k4 = jax.random.split(key, 4)
        stdv = 1.0 / np.sqrt(F_OUT)
        inp = jax.random.normal(k1, (B, N, F_IN), dtype=jnp.float32)
        adj = jax.random.uniform(k2, (B, N, N), dtype=jnp.float32)
        weight = jax.random.uniform(k3, (F_IN, F_OUT), minval=-stdv, maxval=stdv, dtype=jnp.float32)
        bias = jax.random.uniform(k4, (F_OUT,), minval=-stdv, maxval=stdv, dtype=jnp.float32)
        return {'input': inp, 'adj': adj, 'weight': weight, 'bias': bias}
    _L2_gnn_all = _L2_gnn_setup()
    _L2_gnn_in = {k: v for k, v in _L2_gnn_all.items() if k in ('weight', 'bias')}
    del _L2_gnn_all

    def _L3_gnn_setup():
        import jax, jax.numpy as jnp
        import numpy as np
        B, N, D_IN, D_OUT = (16, 1024, 64, 64)
        BN_EPS = 1e-05
        key = jax.random.key(seed)
        k_x, k_adj, k_len, k_w = jax.random.split(key, 4)
        x = jax.random.normal(k_x, (B, N, D_IN), dtype=jnp.float32)
        adj_matrix = jax.random.uniform(k_adj, (B, N, N), dtype=jnp.float32)
        lengths = jax.random.randint(k_len, (B,), N // 2, N + 1)
        mask = (jnp.arange(N)[None, :] < lengths[:, None]).astype(jnp.float32)
        weight = jax.random.normal(k_w, (D_IN, D_OUT), dtype=jnp.float32) * np.sqrt(2.0 / (D_IN + D_OUT))
        bias = jnp.zeros((D_OUT,), dtype=jnp.float32)
        gamma = jnp.ones((D_OUT,), dtype=jnp.float32)
        beta = jnp.zeros((D_OUT,), dtype=jnp.float32)
        return {'x': x, 'adj_matrix': adj_matrix, 'mask': mask, 'weight': weight, 'bias': bias, 'gamma': gamma, 'beta': beta}
    _L3_gnn_all = _L3_gnn_setup()
    _L3_gnn_in = {k: v for k, v in _L3_gnn_all.items() if k in ('weight', 'bias', 'gamma', 'beta')}
    del _L3_gnn_all
    return {'x': x, 'adj': adj, 'nodemask': nodemask, 'L0_gnn_U': _L0_gnn_in['U'], 'L0_gnn_w_scale': _L0_gnn_in['w_scale'], 'L1_gnn_W0': _L1_gnn_in['W0'], 'L1_gnn_b0': _L1_gnn_in['b0'], 'L1_gnn_W1': _L1_gnn_in['W1'], 'L1_gnn_b1': _L1_gnn_in['b1'], 'L1_gnn_W2': _L1_gnn_in['W2'], 'L1_gnn_b2': _L1_gnn_in['b2'], 'L1_gnn_Wout': _L1_gnn_in['Wout'], 'L1_gnn_bout': _L1_gnn_in['bout'], 'L2_gnn_weight': _L2_gnn_in['weight'], 'L2_gnn_bias': _L2_gnn_in['bias'], 'L3_gnn_weight': _L3_gnn_in['weight'], 'L3_gnn_bias': _L3_gnn_in['bias'], 'L3_gnn_gamma': _L3_gnn_in['gamma'], 'L3_gnn_beta': _L3_gnn_in['beta']}

def reference(x, adj, nodemask, L0_gnn_U, L0_gnn_w_scale, L1_gnn_W0, L1_gnn_b0, L1_gnn_W1, L1_gnn_b1, L1_gnn_W2, L1_gnn_b2, L1_gnn_Wout, L1_gnn_bout, L2_gnn_weight, L2_gnn_bias, L3_gnn_weight, L3_gnn_bias, L3_gnn_gamma, L3_gnn_beta):
    import jax
    import jax.numpy as jnp

    def _L0_gnn_ref(x, W, U, w_scale):
        import jax, jax.numpy as jnp
        import numpy as np
        B, N, C, R = (4, 2048, 64, 16)
        EPS = 1e-12
        Ws = 0.5 * (W + jnp.swapaxes(W, -1, -2))
        A = jax.nn.sigmoid(U @ U.T)
        K = Ws * A[None, :, :]
        deg = jnp.maximum(K.sum(axis=-1), EPS)
        d = jax.lax.rsqrt(deg)
        K = K * d[:, :, None] * d[:, None, :]
        return w_scale * jnp.einsum('bnm,bmc->bnc', K, x)

    def _L1_gnn_ref(latent_features, adjacency_matrix, node_mask, W0, b0, W1, b1, W2, b2, Wout, bout):
        import jax, jax.numpy as jnp
        import numpy as np
        NORM = 1.0

        def _glorot(key, shape):
            fan_in, fan_out = shape
            lim = float(np.sqrt(6.0 / (fan_in + fan_out)))
            return jax.random.uniform(key, shape, jnp.float32, -lim, lim)

        def _gcn_layer(h, adj, W, b):
            msg = h @ W + b
            agg = jnp.einsum('bij,bjd->bid', adj, msg) / NORM
            return jax.nn.relu(agg)
        h = _gcn_layer(latent_features, adjacency_matrix, W0, b0)
        h = _gcn_layer(h, adjacency_matrix, W1, b1)
        h = _gcn_layer(h, adjacency_matrix, W2, b2)
        return (h @ Wout + bout) * node_mask

    def _L2_gnn_ref(input, adj, weight, bias):
        import jax, jax.numpy as jnp
        import numpy as np
        B, N, F_IN, F_OUT = (128, 256, 64, 64)
        support = jnp.einsum('bnf,fo->bno', input, weight)
        out = jnp.einsum('bmn,bmo->bno', adj, support)
        return out + bias

    def _L3_gnn_ref(x, adj_matrix, mask, weight, bias, gamma, beta):
        import jax, jax.numpy as jnp
        import numpy as np
        B, N, D_IN, D_OUT = (16, 1024, 64, 64)
        BN_EPS = 1e-05
        y = jnp.matmul(adj_matrix, x) + x
        y = jnp.matmul(y, weight) + bias
        norm = jnp.linalg.norm(y, axis=2, keepdims=True)
        y = y / jnp.maximum(norm, 1e-12)
        m = mask[..., None]
        cnt = jnp.sum(mask)
        mean = jnp.sum(y * m, axis=(0, 1)) / cnt
        var = jnp.sum((y - mean) ** 2 * m, axis=(0, 1)) / cnt
        y = ((y - mean) / jnp.sqrt(var + BN_EPS) * gamma + beta) * m
        return jax.nn.relu(y)
    x = _layernorm(x + _L0_gnn_ref(x, adj, L0_gnn_U, L0_gnn_w_scale), axis=-1)
    x = _layernorm(x + _L1_gnn_ref(x, adj, nodemask[..., None], L1_gnn_W0, L1_gnn_b0, L1_gnn_W1, L1_gnn_b1, L1_gnn_W2, L1_gnn_b2, L1_gnn_Wout, L1_gnn_bout), axis=-1)
    x = _layernorm(x + _L2_gnn_ref(x, adj, L2_gnn_weight, L2_gnn_bias), axis=-1)
    x = _layernorm(x + _L3_gnn_ref(x, adj, nodemask, L3_gnn_weight, L3_gnn_bias, L3_gnn_gamma, L3_gnn_beta), axis=-1)
    return x

_drawn_inputs = setup_inputs


def setup_inputs(seed=0):
    import zlib

    import numpy as np

    out = dict(_drawn_inputs(seed))
    spreads = {'L1_gnn_b0': (0.0, 0.1),
     'L1_gnn_b1': (0.0, 0.1),
     'L1_gnn_b2': (0.0, 0.1),
     'L1_gnn_bout': (0.0, 0.1),
     'L3_gnn_bias': (0.0, 0.711),
     'L3_gnn_gamma': (1.0, 0.2),
     'L3_gnn_beta': (0.0, 0.1)}
    factors = {'L0_gnn_U': 64.0}
    for name, (base, spread) in spreads.items():
        noise = np.random.default_rng([zlib.crc32(name.encode()), seed]).standard_normal(out[name].shape)
        drawn = base * np.exp(spread * noise) if base else spread * noise
        out[name] = jnp.asarray(drawn.astype(out[name].dtype))
    for name, factor in factors.items():
        out[name] = (out[name] * factor).astype(out[name].dtype)
    return out
```

```python
import concourse.bass as bass
from concourse import mybir
from contextlib import ExitStack

F32 = mybir.dt.float32
F16 = mybir.dt.float16
BF16 = mybir.dt.bfloat16
ALU = mybir.AluOpType
ACT = mybir.ActivationFunctionType
AX = mybir.AxisListType

P = 128
B, N, C, H = 8, 2048, 64, 128
T = N // P
TP = T // 2
W = 512
Q = N // W
TQ = W // P
R = 16
NC_ = T * C
LAYERS = 3
LN_EPS = 1e-5
DEG_EPS = 1e-12
BN_EPS = 1e-5
NORM_FLOOR = 1e-12


def build(nc, x_in, adj, mask_in, ut, wscale, w0, w1, w2, wout, l2w, l3w, b0, b1, b2, bout, l2b, l3b,
          gamma, beta, ident_in, fold_in, pick_in, out):
    ctx = ExitStack()
    with ctx:
        def sb(name, shape, dt=F32):
            return ctx.enter_context(nc.sbuf_tensor(name, shape, dt))

        def sem(name):
            return ctx.enter_context(nc.semaphore(name))

        def sems(name, n):
            return [sem(f"{name}{i}") for i in range(n)]

        y_all = nc.dram_tensor("y_all", (B, P, NC_), F32).ap()
        x3_all = nc.dram_tensor("x3_all", (B, P, NC_), F32).ap()

        at = sb("at", [P, 2, T, N], F16)
        pair = sb("pair", [P, 2, 2, N], F16)
        col_ring = sb("col_ring", [P, Q, TQ, P])
        row_ring = sb("row_ring", [P, Q, W])
        sym = sb("sym", [P, 2, W])
        gate = sb("gate", [P, 2, W])
        kf = sb("kf", [P, 2, W])
        ht = sb("ht", [P, N])
        x = sb("x", [P, NC_])
        xs = sb("xs", [P, T, P], F16)
        vs = sb("vs", [P, 2, P], F16)
        vf = sb("vf", [P, 2, C])
        ul = sb("ul", [P, N], BF16)
        ur = sb("ur", [P, N], BF16)
        ident = sb("ident", [P, P])
        ident16 = sb("ident16", [P, P], F16)
        fold = sb("fold", [P, C])
        pick = sb("pick", [P, 6])
        w0s = sb("w0s", [P, H])
        w1s = sb("w1s", [H, H])
        w2s = sb("w2s", [H, H])
        wouts = sb("wouts", [H, C])
        l2ws = sb("l2ws", [P, C])
        l3ws = sb("l3ws", [P, C])
        bias = sb("bias", [P, LAYERS, H])
        cbias = sb("cbias", [P, 5, C])
        mask = sb("mask", [P, B * T])
        wsc = sb("wsc", [P, 1])
        ones = sb("ones", [P, P])
        part = sb("part", [P, 2, Q])
        deg = sb("deg", [P, 2, 2])
        half_neg = sb("half_neg", [P, C])
        d = sb("d", [P, T])
        wd = sb("wd", [P, T])
        mean = sb("mean", [P, T])
        rstd = sb("rstd", [P, 2, T])
        tmp = kf[:, :, :].rearrange("p a w -> p (a w)")
        sq = sym[:, :, :].rearrange("p a w -> p (a w)")

        acc = ctx.enter_context(nc.psum_tensor("acc", [P, Q, W], F32))
        side = ctx.enter_context(nc.psum_tensor("side", [P, 2, 2, W], F32))
        turn, uu = side[:, :, 0, :], side[:, :, 1, :]

        consts_in = sem("consts_in")
        const_made = sem("const_made")
        u_step = sem("u_step")
        col_in = sems("col_in", Q)
        row_in = sems("row_in", Q)
        x_in_done = sem("x_in_done")
        turned = sems("turned", Q)
        uu_done = sems("uu_done", Q)
        at_hi = sems("at_hi", Q)
        at_lo = sems("at_lo", Q)
        row_used = sems("row_used", Q)
        gated = sems("gated", Q)
        k_done = sems("k_done", Q)
        k_hi = sems("k_hi", Q)
        k_lo = sems("k_lo", Q)
        row_hi = sems("row_hi", Q)
        deg_sum = sem("deg_sum")
        deg_done = sem("deg_done")
        deg_step = sem("deg_step")
        v_done = sem("v_done")
        slot_used = sems("slot_used", 2)
        at_used = sem("at_used")
        prod3 = sem("prod3")
        evac = sem("evac")
        proj = sem("proj")
        xt_done = sem("xt_done")
        xt_sb = sem("xt_sb")
        msg_mm = sem("msg_mm")
        msg_f = sem("msg_f")
        msg_hi = sem("msg_hi")
        msg_lo = sem("msg_lo")
        agg = sem("agg")
        relu = sem("relu")
        wd_done = sem("wd_done")
        e_scaled = sem("e_scaled")
        e_masked = sem("e_masked")
        e_sum = sem("e_sum")
        e_total = sem("e_total")
        e_mean = sem("e_mean")
        e_cent = sem("e_cent")
        e_sq = sem("e_sq")
        e_var = sem("e_var")
        e_veps = sem("e_veps")
        e_rstd = sem("e_rstd")
        e_x = sem("e_x")
        x_hi = sem("x_hi")
        x_lo = sem("x_lo")
        y_bias = sem("y_bias")
        y_sq = sem("y_sq")
        y_var = sem("y_var")
        y_floor = sem("y_floor")
        y_rstd = sem("y_rstd")
        y_done = sem("y_done")
        y_out = sem("y_out")
        x3_out = sem("x3_out")
        f_in = sem("f_in")
        f_dve = sem("f_dve")
        f_act = sem("f_act")
        f_pe = sem("f_pe")
        f_pool = sem("f_pool")
        f_out = sem("f_out")

        EPI = 3
        HALF = T // 2
        HC = HALF * C

        def half(ap, h):
            return ap[:, h * HC:(h + 1) * HC]

        def tiles(ap, h):
            return half(ap, h).rearrange("p (t c) -> p t c", c=C)

        def spread(ap, h):
            return ap[:, h * HALF:(h + 1) * HALF].unsqueeze(2).broadcast_to([P, HALF, C])

        def over_tiles(ap, n, w):
            return ap.unsqueeze(1).broadcast_to([P, n, w])

        def at_q(part_, i, q):
            return at[:, part_, bass.ds(i, 1), q * W:(q + 1) * W].rearrange("p a w -> p (a w)")

        def natural(e, h):
            bank = turn[:, h, :] if e == 1 else acc[:, h, :]
            return bank.rearrange("p (t c) -> p t c", c=C)

        N_CONSTS = 7 + 6 + P // R + 3 + 5 + 1
        U_STEPS = 13
        FINAL_MU = 1 + B + 3
        FINAL_HEAD = FINAL_MU + 3 * B + 3
        FINAL_STEPS = 10

        OPEN = 1

        def start_at_one(eng, *opened):
            for s in opened:
                eng.sem_inc(s, OPEN)

        block = ctx.enter_context(nc.Block())

        @block.sync
        def _(sp):
            for dst, src in ((ident, ident_in), (fold, fold_in), (pick, pick_in), (w1s, w1),
                             (w2s, w2), (wouts, wout), (mask, mask_in)):
                sp.dma_start(dst[:, :], src).then_inc(consts_in, 16)
            for h in range(2):
                sp.dma_start(w0s[h * C:(h + 1) * C, :], w0).then_inc(consts_in, 16)
                sp.dma_start(l2ws[h * C:(h + 1) * C, :], l2w).then_inc(consts_in, 16)
                sp.dma_start(l3ws[h * C:(h + 1) * C, :], l3w).then_inc(consts_in, 16)
            for g in range(P // R):
                sp.dma_start(ht[g * R:(g + 1) * R, :], ut).then_inc(consts_in, 16)
            for n, v in enumerate((b0, b1, b2)):
                sp.dma_start(bias[:, n, :], v.partition_broadcast(P)).then_inc(consts_in, 16)
            for n, v in enumerate((bout, l2b, l3b, gamma, beta)):
                sp.dma_start(cbias[:, n, :], v.partition_broadcast(P)).then_inc(consts_in, 16)
            sp.dma_start(wsc[:, :], wscale.partition_broadcast(P)).then_inc(consts_in, 16)
            with sp.Fori(0, B) as b:
                with sp.Fori(0, T) as i:
                    for q in range(Q):
                        sp.wait_ge(turned[q], b * T + i + OPEN)
                        sp.dma_start(col_ring[:, q, :, :],
                                     adj[bass.ds(b, 1), q * W:(q + 1) * W, bass.ds(i * P, P)]
                                     .rearrange("a (t p) c -> p (a t) c", p=P)).then_inc(col_in[q], 16)
                        sp.wait_ge(row_used[q], b * 2 * T + i + OPEN)
                        sp.dma_start(row_ring[:, q, :],
                                     adj[bass.ds(b, 1), bass.ds(i * P, P), q * W:(q + 1) * W]
                                     .rearrange("a p c -> p (a c)")).then_inc(row_in[q], 16)
                with sp.Fori(0, T) as i:
                    for q in range(Q):
                        sp.wait_ge(row_used[q], b * 2 * T + T + i + OPEN)
                        sp.dma_start(row_ring[:, q, :],
                                     adj[bass.ds(b, 1), bass.ds(i * P, P), q * W:(q + 1) * W]
                                     .rearrange("a p c -> p (a c)")).then_inc(row_in[q], 16)
            yf = at[:, 0, 0:8, :].rearrange("p a n -> p (a n)").bitcast(F32)
            xf = at[:, 0, 8:16, :].rearrange("p a n -> p (a n)").bitcast(F32)
            sp.wait_ge(y_out, 16 * B)
            sp.wait_ge(x3_out, 16 * (B + 1))
            sp.wait_ge(at_used, B * T + OPEN)
            sp.dma_start(yf.rearrange("p (b n) -> p b n", b=B), y_all.rearrange("b p n -> p b n")).then_inc(f_in, 16)
            sp.dma_start(xf.rearrange("p (b n) -> p b n", b=B), x3_all.rearrange("b p n -> p b n")).then_inc(f_in, 16)
            for b in range(B):
                sp.wait_ge(f_dve, FINAL_HEAD + FINAL_STEPS * (b + 1))
                sp.dma_start(out[b], xf[:, b * NC_:(b + 1) * NC_]).then_inc(f_out, 16)
            sp.wait_ge(f_out, 16 * B)


        @block.tensor
        def _(pe):
            def stripe_units(n, i):
                for q in range(Q):
                    pe.wait_ge(col_in[q], (n + 1) * 16)
                    before, more = (q + 2) % Q, int(q >= 2)
                    pe.wait_ge(at_lo[before], n + more + OPEN)
                    for t in range(TQ):
                        mm = nc.tensor.transpose(turn[:, q % 2, t * P:(t + 1) * P], col_ring[:, q, t, :], ident[:, :])
                    mm.then_inc(turned[q], 1)
                    pe.wait_ge(gated[before], n + more + OPEN)
                    nc.tensor.matmul(uu[:, q % 2, :], ul[:, bass.ds(i * P, P)], ur[:, q * W:(q + 1) * W],
                                     start=True, stop=True).then_inc(uu_done[q], 1)

            def k_product(n, s, first=False, last=False):
                pe.wait_ge(v_done, n + 1)
                for q in range(Q):
                    pe.wait_ge(k_lo[q], n + 1 + OPEN)
                    for h in range(2):
                        mm = nc.tensor.matmul(acc[:, q, :], vs[:, s, :], pair[:, s, h, q * W:(q + 1) * W],
                                              start=(first and h == 0), stop=(last and h == 1))
                mm.then_inc(slot_used[s], 1)

            def project(e, weights, lo, hi):
                for t in range(lo, hi):
                    mm = nc.tensor.matmul(natural(e, t // HALF)[:, t % HALF, :], ht[:, t * P:(t + 1) * P],
                                          weights, start=True, stop=True)
                    if t % HALF == HALF - 1:
                        mm.then_inc(proj, 1)

            def project_all(e, b, weights):
                pe.wait_ge(evac, b * 3 * Q + max(e - 1, 0) * Q + Q)
                project(e, weights, 0, T)

            def messages(b, k, c):
                weights = (w0s, w1s, w2s)[k]
                if k > 0:
                    pe.wait_ge(relu, (b * LAYERS + k - 1) * Q + c + 1)
                n = (b * LAYERS + k) * Q + c
                if k > 0 or c >= 2:
                    pe.wait_ge(msg_f, n - 1)
                elif c == 0:
                    pe.wait_ge(gated[3], (b + 1) * T + OPEN)
                for t in range(TQ):
                    tile = c * TQ + t
                    rows, a, to = slice(0, P), tile * P, turn[:, c % 2, t * H:(t + 1) * H]
                    if k == 0:
                        o = tile % 2
                        rows, a = slice(o * C, o * C + C), tile // 2 * P
                        to = side[:, c % 2, o, t // 2 * H:(t // 2 + 1) * H]
                    mm = nc.tensor.matmul(to, ht[rows, a:a + P], weights[rows, :], start=True, stop=True)
                mm.then_inc(msg_mm, 1)

            def agg_step(b, k, c, j, start=False, stop=False):
                s = k % 2
                hi = pair[:, s, 0, bass.ds(j * P, P)]
                lo = pair[:, s, 1, bass.ds(j * P, P)]
                nc.tensor.matmul(acc[:, c, :], hi, at_q(0, j, c), start=start, stop=False)
                nc.tensor.matmul(acc[:, c, :], hi, at_q(1, j, c), start=False, stop=False)
                return nc.tensor.matmul(acc[:, c, :], lo, at_q(0, j, c), start=False, stop=stop)

            def aggregate(b, k, c):
                agg_step(b, k, c, 0, start=True)
                with pe.Fori(1, T - 1, 2) as j:
                    agg_step(b, k, c, j)
                    agg_step(b, k, c, j + 1)
                agg_step(b, k, c, T - 1, stop=True).then_inc(agg, 1)

            def row_product(b, i, s, q_first=False, last=False):
                for q in range(Q):
                    pe.wait_ge(row_used[q], b * 2 * T + T + i + 1 + OPEN)
                    for h in range(2):
                        mm = nc.tensor.matmul(acc[:, q, :], xs[:, bass.ds(i, 1), :].rearrange("p a c -> p (a c)"),
                                              pair[:, s, h, q * W:(q + 1) * W],
                                              start=(q_first and h == 0), stop=(last and h == 1))
                mm.then_inc(slot_used[s], 1)

            def at_product(i, first=False):
                xi = xs[:, bass.ds(i, 1), :].rearrange("p a c -> p (a c)")
                for q in range(Q):
                    for h in range(2):
                        mm = nc.tensor.matmul(acc[:, q, :], xi, at_q(h, i, q), start=(first and h == 0), stop=False)
                mm.then_inc(at_used, 1)

            start_at_one(pe, *turned, *slot_used, at_used)
            pe.wait_ge(u_step, U_STEPS)
            pe.wait_ge(const_made, 1)
            with pe.Fori(0, B) as b:
                stripe_units(b * T, 0)
                stripe_units(b * T + 1, 1)
                pe.wait_ge(y_bias, b * 2 + OPEN)
                k_product(b * T, 0, first=True)
                with pe.Fori(1, TP) as jj:
                    stripe_units(b * T + jj * 2, jj * 2)
                    k_product(b * T + jj * 2 - 1, 1)
                    stripe_units(b * T + jj * 2 + 1, jj * 2 + 1)
                    k_product(b * T + jj * 2, 0)
                k_product(b * T + T - 1, 1, last=True)
                project_all(0, b, fold[:, :])
                for h in range(2):
                    pe.wait_ge(e_x, b * 2 * EPI + h + 1)
                    for t in range(TQ):
                        a = (h * TQ + t) * 2 * C
                        mm = nc.tensor.transpose(turn[:, h, t * P:(t + 1) * P], x[:, a:a + 2 * C], ident[:, :])
                    mm.then_inc(xt_done, 1)
                pe.wait_ge(xt_sb, b * 2 + 2)
                for c in range(Q):
                    messages(b, 0, c)
                for k in range(LAYERS):
                    m = (b * LAYERS + k) * Q
                    for j in range(0, T, TQ):
                        if j == T - TQ and k > 0:
                            messages(b, k, Q - 1)
                        pe.wait_ge(msg_lo, m + j // TQ + 1)
                        for jj in range(j, j + TQ):
                            mm = agg_step(b, k, 0, jj, start=(jj == 0), stop=(jj == T - 1))
                    mm.then_inc(agg, 1)
                    for c in range(1, Q):
                        aggregate(b, k, c)
                        if k < LAYERS - 1:
                            messages(b, k + 1, c - 1)
                for c in range(Q):
                    pe.wait_ge(relu, (b * LAYERS + LAYERS - 1) * Q + c + 1)
                    if c == 0:
                        pe.wait_ge(msg_f, (b + 1) * LAYERS * Q)
                    project(1, wouts[:, :], c * TQ, (c + 1) * TQ)
                pe.wait_ge(x_lo, b * 4 + 2 + OPEN)
                row_product(b, 0, 1, q_first=True)
                row_product(b, 1, 0)
                with pe.Fori(1, TP - 1) as jj:
                    row_product(b, jj * 2, 1)
                    row_product(b, jj * 2 + 1, 0)
                row_product(b, T - 2, 1)
                row_product(b, T - 1, 0, last=True)
                project_all(2, b, l2ws[:, :])
                pe.wait_ge(x_lo, b * 4 + 4 + OPEN)
                at_product(0, first=True)
                with pe.Fori(1, T) as i:
                    at_product(i)
                for t in range(T):
                    mm = nc.tensor.matmul(acc[:, t // TQ, t % TQ * P:(t % TQ + 1) * P], xs[:, t, :], ident16[:, :],
                                          start=False, stop=(t % TQ == TQ - 1))
                mm.then_inc(prod3, 1)
                project_all(3, b, l3ws[:, :])

            yf = at[:, 0, 0:8, :].rearrange("p a n -> p (a n)").bitcast(F32)
            sqf = at[:, 1, 0:8, :].rearrange("p a n -> p (a n)").bitcast(F32)
            pe.wait_ge(f_dve, 1)
            nc.tensor.matmul(turn[:, 0, 0:1], ones[:, :], d[:, 0:1], start=True, stop=True).then_inc(f_pe, 1)
            for b in range(B):
                pe.wait_ge(f_dve, 2 + b)
                for h in range(2):
                    a = (2 * b + h) * HC
                    mm = nc.tensor.matmul(acc[:, 0, :], ones[:, :], sqf[:, a:a + HC], start=(a == 0),
                                          stop=(a == (2 * B - 1) * HC))
            mm.then_inc(f_pe, 1)
            for b in range(B):
                pe.wait_ge(f_dve, FINAL_MU + 3 * (b + 1))
                for h in range(2):
                    a = (2 * b + h) * HC
                    mm = nc.tensor.matmul(acc[:, 1, :], ones[:, :], sqf[:, a:a + HC], start=(a == 0),
                                          stop=(a == (2 * B - 1) * HC))
            mm.then_inc(f_pe, 1)

        @block.scalar
        def _(act):
            def head(b, i, q):
                n = b * T + i
                act.wait_ge(turned[q], n + 1 + OPEN)
                if q == 0:
                    act.wait_ge(at_used, b * T + OPEN)
                nc.scalar.activation(at_q(0, i, q), turn[:, q % 2, :], ACT.Copy).then_inc(at_hi[q], 1)
                act.wait_ge(uu_done[q], n + 1)
                act.wait_ge(k_done[(q + 2) % Q], n + int(q >= 2) + OPEN)
                nc.scalar.activation(gate[:, q % 2, :], uu[:, q % 2, :], ACT.Sigmoid).then_inc(gated[q], 1)

            def k_high(b, jj, n, s, q):
                act.wait_ge(k_done[q], n + 1 + OPEN)
                if q == 0:
                    act.wait_ge(slot_used[s], b * T + jj + OPEN)
                nc.scalar.activation(pair[:, s, 0, q * W:(q + 1) * W], kf[:, q % 2, :], ACT.Copy).then_inc(k_hi[q], 1)

            def pair_of_stripes(b, jj, last):
                for k in range(2 * Q):
                    nk = k + 1
                    if nk < 2 * Q:
                        head(b, jj * 2 + nk // Q, nk % Q)
                    elif not last:
                        head(b, jj * 2 + 2, 0)
                    k_high(b, jj, b * T + jj * 2 + k // Q, k // Q, k % Q)

            def norm_steps(b, e):
                for h in range(2):
                    act.wait_ge(e_cent, b * 2 * EPI + 2 * e + h + 1)
                    nc.scalar.activation(half(sq, h), half(tmp, h), ACT.Square).then_inc(e_sq, 1)

            def x_high(b, e):
                for h in range(2):
                    act.wait_ge(e_x, b * 2 * EPI + 2 * e + h + 1)
                    nc.scalar.activation(xs[:, h * HALF:(h + 1) * HALF, 0:C], tiles(x, h), ACT.Copy).then_inc(x_hi, 1)

            def evacuate(b, n):
                if n == 0:
                    act.wait_ge(slot_used[1], b * T + TP + OPEN)
                elif n == 1:
                    act.wait_ge(slot_used[0], (b + 1) * T + OPEN)
                else:
                    act.wait_ge(prod3, b + 1)
                for c in range(Q):
                    nc.scalar.activation(ht[:, c * W:(c + 1) * W], acc[:, c, :], ACT.Copy).then_inc(evac, 1)

            def message_high(b, k, c):
                n = (b * LAYERS + k) * Q + c
                act.wait_ge(msg_f, n + 1)
                if c == 0:
                    if k < 2:
                        act.wait_ge(slot_used[k], b * T + TP + OPEN)
                    else:
                        act.wait_ge(agg, (b * LAYERS + 1) * Q)
                nc.scalar.activation(pair[:, k % 2, 0, c * W:(c + 1) * W], kf[:, c % 2, :], ACT.Copy).then_inc(msg_hi, 1)

            def row_high(b, jj, i, s, q):
                act.wait_ge(row_in[q], (b * 2 * T + T + i + 1) * 16)
                if q == 0:
                    act.wait_ge(agg, (b * LAYERS + (3 if s == 0 else 2)) * Q)
                    act.wait_ge(slot_used[s], b * T + TP + jj + OPEN)
                nc.scalar.activation(pair[:, s, 0, q * W:(q + 1) * W], row_ring[:, q, :], ACT.Copy).then_inc(row_hi[q], 1)

            start_at_one(act, *gated)
            act.sem_inc(x3_out, 16)
            act.wait_ge(consts_in, N_CONSTS * 16)
            nc.scalar.activation(ident16[:, :], ident[:, :], ACT.Copy).then_inc(const_made, 1)
            with act.Fori(0, B) as b:
                act.wait_ge(x3_out, (b + 1) * 16)
                act.wait_ge(x_lo, b * 4 + OPEN)
                act.dma_start(x[:, :], x_in[bass.ds(b, 1), :, :].rearrange("a p n -> p (a n)")).then_inc(x_in_done, 16)
                head(b, 0, 0)
                with act.Fori(0, TP - 1) as jj:
                    pair_of_stripes(b, jj, False)
                pair_of_stripes(b, TP - 1, True)
                evacuate(b, 0)
                norm_steps(b, 0)
                for h in range(2):
                    act.wait_ge(xt_done, b * 2 + h + 1)
                    nc.scalar.activation(ht[:, h * W:(h + 1) * W], turn[:, h, :], ACT.Copy).then_inc(xt_sb, 1)
                for c in range(Q):
                    message_high(b, 0, c)
                for k in range(LAYERS):
                    for c in range(Q):
                        if k == 2 and c == 0:
                            for q in range(Q):
                                row_high(b, 0, 0, 1, q)
                        act.wait_ge(agg, (b * LAYERS + k) * Q + c + 1)
                        nc.scalar.activation(ht[:, c * W:(c + 1) * W], acc[:, c, :], ACT.Relu).then_inc(relu, 1)
                        if k < LAYERS - 1 and c > 0:
                            message_high(b, k + 1, c - 1)
                    if k < LAYERS - 1:
                        message_high(b, k + 1, Q - 1)
                for q in range(Q):
                    row_high(b, 0, 1, 0, q)
                norm_steps(b, 1)
                x_high(b, 1)
                with act.Fori(1, TP) as jj:
                    for s in range(2):
                        for q in range(Q):
                            row_high(b, jj, jj * 2 + s, 1 - s, q)
                evacuate(b, 1)
                norm_steps(b, 2)
                x_high(b, 2)
                act.dma_start(x3_all[bass.ds(b, 1), :, :].rearrange("a p n -> p (a n)"), x[:, :]).then_inc(x3_out, 16)
                evacuate(b, 2)
                for h in range(2):
                    act.wait_ge(y_bias, b * 2 + h + 1 + OPEN)
                    nc.scalar.activation(half(sq, h), half(tmp, h), ACT.Square).then_inc(y_sq, 1)
                act.wait_ge(y_done, b * 2 + 2)
                act.dma_start(y_all[bass.ds(b, 1), :, :].rearrange("a p n -> p (a n)"), tmp).then_inc(y_out, 16)
            xf = at[:, 0, 8:16, :].rearrange("p a n -> p (a n)").bitcast(F32)
            sqf = at[:, 1, 0:8, :].rearrange("p a n -> p (a n)").bitcast(F32)
            with act.Fori(0, B) as b:
                act.wait_ge(f_dve, FINAL_HEAD + FINAL_STEPS * b + 7)
                nc.scalar.activation(sqf[:, bass.ds(b * NC_, NC_)], xf[:, bass.ds(b * NC_, NC_)], ACT.Square)\
                  .then_inc(f_act, 1)

        @block.vector
        def _(dve):
            def unit(b, jj, s, q):
                i = jj * 2 + s
                n = b * T + i
                dve.wait_ge(row_in[q], (b * 2 * T + i + 1) * 16)
                dve.wait_ge(at_hi[q], n + 1)
                nc.vector.tensor_tensor(sym[:, q % 2, :], row_ring[:, q, :], turn[:, q % 2, :], ALU.add)\
                  .then_inc(row_used[q], 1)
                nc.vector.tensor_tensor(at_q(1, i, q), turn[:, q % 2, :], at_q(0, i, q), ALU.subtract)\
                  .then_inc(at_lo[q], 1)
                dve.wait_ge(row_used[q], b * 2 * T + i + 1 + OPEN)
                dve.wait_ge(gated[q], n + 1 + OPEN)
                dve.wait_ge(k_lo[(q + 2) % Q], n + int(q >= 2) + OPEN)
                nc.vector.scalar_tensor_tensor(kf[:, q % 2, :], sym[:, q % 2, :], 1.0, gate[:, q % 2, :], ALU.mult,
                                               ALU.mult, accum_out=part[:, s, q:q + 1]).then_inc(k_done[q], 1)

            def degree(n, s):
                for q in range(Q):
                    dve.wait_ge(k_done[q], n + 1 + OPEN)
                nc.vector.tensor_reduce(deg[:, s, 0:1], part[:, s, :], AX.X, ALU.add).then_inc(deg_sum, 1)
                dve.wait_ge(deg_sum, n + 1)
                nc.vector.tensor_scalar(deg[:, s, 1:2], deg[:, s, 0:1], 0.5, DEG_EPS, ALU.mult, ALU.max)\
                  .then_inc(deg_done, 1)

            def norm(b, e):
                v = b * 2 * EPI + 2 * e + 1
                for h in range(2):
                    dve.wait_ge(proj, b * 8 + 2 * e + h + 1)
                    if e == 0:
                        nc.vector.tensor_tensor(tiles(tmp, h), natural(e, h), spread(wd, h), ALU.mult).then_inc(e_scaled, 1)
                    else:
                        nc.vector.tensor_tensor(tiles(tmp, h), natural(e, h),
                                                over_tiles(cbias[:, e - 1, :], HALF, C), ALU.add).then_inc(e_scaled, 1)
                if e == 1:
                    for h in range(2):
                        dve.wait_ge(e_scaled, v + h)
                        m = mask[:, bass.ds(b * T + h * HALF, HALF)].unsqueeze(2).broadcast_to([P, HALF, C])
                        nc.vector.tensor_tensor(tiles(tmp, h), tiles(tmp, h), m, ALU.mult).then_inc(e_masked, 1)
                for h in range(2):
                    dve.wait_ge(e_scaled, v + h)
                    if e == 1:
                        dve.wait_ge(e_masked, b * 2 + h + 1)
                    nc.vector.tensor_tensor(half(tmp, h), half(tmp, h), half(x, h), ALU.add).then_inc(e_sum, 1)
                for h in range(2):
                    dve.wait_ge(e_sum, v + h)
                    nc.vector.tensor_reduce(mean[:, h * HALF:(h + 1) * HALF], tiles(tmp, h), AX.X, ALU.add)\
                      .then_inc(e_total, 1)
                for h in range(2):
                    m = mean[:, h * HALF:(h + 1) * HALF]
                    dve.wait_ge(e_total, v + h)
                    nc.vector.tensor_scalar(m, m, -1.0 / C, None, ALU.mult).then_inc(e_mean, 1)
                for h in range(2):
                    dve.wait_ge(e_mean, v + h)
                    nc.vector.tensor_tensor(tiles(tmp, h), tiles(tmp, h), spread(mean, h), ALU.add).then_inc(e_cent, 1)
                for h in range(2):
                    dve.wait_ge(e_sq, v + h)
                    nc.vector.tensor_reduce(rstd[:, 0, h * HALF:(h + 1) * HALF], tiles(sq, h), AX.X, ALU.add)\
                      .then_inc(e_var, 1)
                for h in range(2):
                    r = rstd[:, 0, h * HALF:(h + 1) * HALF]
                    dve.wait_ge(e_var, v + h)
                    nc.vector.tensor_scalar(r, r, 1.0 / C, LN_EPS, ALU.mult, ALU.add).then_inc(e_veps, 1)
                for h in range(2):
                    dve.wait_ge(e_rstd, v + h)
                    dve.wait_ge(e_cent, v + h)
                    nc.vector.tensor_tensor(tiles(x, h), tiles(tmp, h), spread(rstd[:, 1, :], h), ALU.mult).then_inc(e_x, 1)

            def x_low(b, e):
                for h in range(2):
                    dve.wait_ge(x_hi, b * 4 + 2 * (e - 1) + h + 1)
                    s = slice(h * HALF, (h + 1) * HALF)
                    nc.vector.tensor_tensor(xs[:, s, C:P], tiles(x, h), xs[:, s, 0:C], ALU.subtract).then_inc(x_lo, 1)

            def message(b, k, c):
                n = (b * LAYERS + k) * Q + c
                dve.wait_ge(msg_mm, n + 1)
                if c >= 2:
                    dve.wait_ge(msg_lo, n - 1)
                if k == 0:
                    bank = side[:, c % 2, :, 0:W // 2].rearrange("p o (u h) -> p u o h", h=H)
                else:
                    bank = turn[:, c % 2, :].rearrange("p (u o h) -> p u o h", o=2, h=H)
                nc.vector.tensor_tensor(kf[:, c % 2, :].rearrange("p (u o h) -> p u o h", o=2, h=H), bank,
                                        bias[:, k, :].unsqueeze(1).unsqueeze(1).broadcast_to([P, 2, 2, H]),
                                        ALU.add).then_inc(msg_f, 1)
                dve.wait_ge(msg_f, n + 1)
                dve.wait_ge(msg_hi, n + 1)
                cols = slice(c * W, (c + 1) * W)
                nc.vector.tensor_tensor(pair[:, k % 2, 1, cols], kf[:, c % 2, :], pair[:, k % 2, 0, cols],
                                        ALU.subtract).then_inc(msg_lo, 1)

            def row_low(b, i, s, q):
                dve.wait_ge(row_hi[q], b * T + i + 1)
                cols = slice(q * W, (q + 1) * W)
                nc.vector.tensor_tensor(pair[:, s, 1, cols], row_ring[:, q, :], pair[:, s, 0, cols], ALU.subtract)\
                  .then_inc(row_used[q], 1)

            start_at_one(dve, *row_used, *at_lo, *k_done, x_lo, y_bias)
            u = [0]

            def u_next(ins):
                u[0] += 1
                ins.then_inc(u_step, 1)
                dve.wait_ge(u_step, u[0])

            u_next(nc.vector.memset(ones[:, :], 1.0))
            u_next(nc.vector.memset(half_neg[:, :], -0.5))
            dve.wait_ge(consts_in, N_CONSTS * 16)
            u1 = pair[:, 0, 0, :].bitcast(BF16)
            u_next(nc.vector.tensor_copy(u1, ht[:, :]))
            for lr, dst in ((0, ul), (1, ur)):
                u_next(nc.vector.tensor_scalar(dst[:, :], u1, pick[:, 3 * lr:3 * lr + 1], None, ALU.mult))
            for n in (1, 2):
                u_next(nc.vector.tensor_tensor(ht[:, :], ht[:, :], u1, ALU.subtract))
                u_next(nc.vector.tensor_copy(u1, ht[:, :]))
                for lr, dst in ((0, ul), (1, ur)):
                    u_next(nc.vector.scalar_tensor_tensor(dst[:, :], u1, pick[:, 3 * lr + n:3 * lr + n + 1],
                                                          dst[:, :], ALU.mult, ALU.add))
            assert u[0] == U_STEPS

            with dve.Fori(0, B) as b:
                with dve.Fori(0, TP) as jj:
                    for s in range(2):
                        for q in range(Q):
                            unit(b, jj, s, q)
                        degree(b * T + jj * 2 + s, s)
                dve.wait_ge(v_done, (b + 1) * T)
                nc.vector.tensor_scalar(wd[:, :], d[:, :], wsc[:, :], 0.5, ALU.mult, ALU.mult).then_inc(wd_done, 1)
                dve.wait_ge(wd_done, b + 1)
                norm(b, 0)
                for c in range(Q):
                    message(b, 0, c)
                for k in range(1, LAYERS):
                    for c in range(Q):
                        message(b, k, c)
                for i in range(2):
                    for q in range(Q):
                        row_low(b, i, 1 - i, q)
                norm(b, 1)
                x_low(b, 1)
                with dve.Fori(1, TP) as jj:
                    for s in range(2):
                        for q in range(Q):
                            row_low(b, jj * 2 + s, 1 - s, q)
                norm(b, 2)
                x_low(b, 2)
                for h in range(2):
                    dve.wait_ge(proj, b * 8 + 6 + h + 1)
                    nc.vector.tensor_tensor(tiles(tmp, h), natural(3, h), over_tiles(cbias[:, 2, :], HALF, C),
                                            ALU.add).then_inc(y_bias, 1)
                for h in range(2):
                    dve.wait_ge(y_sq, b * 2 + h + 1)
                    nc.vector.tensor_reduce(rstd[:, 0, h * HALF:(h + 1) * HALF], tiles(sq, h), AX.X, ALU.add)\
                      .then_inc(y_var, 1)
                for h in range(2):
                    r = rstd[:, 0, h * HALF:(h + 1) * HALF]
                    dve.wait_ge(y_var, b * 2 + h + 1)
                    nc.vector.tensor_scalar(r, r, NORM_FLOOR ** 2, None, ALU.max).then_inc(y_floor, 1)
                for h in range(2):
                    dve.wait_ge(y_rstd, b * 2 + h + 1)
                    nc.vector.tensor_tensor(tiles(tmp, h), tiles(tmp, h), spread(rstd[:, 1, :], h), ALU.mult)\
                      .then_inc(y_done, 1)
                dve.wait_ge(y_out, (b + 1) * 16)

            yf = at[:, 0, 0:8, :].rearrange("p a n -> p (a n)").bitcast(F32)
            xf = at[:, 0, 8:16, :].rearrange("p a n -> p (a n)").bitcast(F32)
            sqf = at[:, 1, 0:8, :].rearrange("p a n -> p (a n)").bitcast(F32)
            step = [0]

            def link(ins, wait=True):
                step[0] += 1
                ins.then_inc(f_dve, 1)
                if wait:
                    dve.wait_ge(f_dve, step[0])

            def graph(ap, b):
                return ap[:, bass.ds(b * NC_, NC_)]

            def graph_tiles(ap, b):
                return graph(ap, b).rearrange("p (t c) -> p t c", c=C)

            def graph_mask(b):
                return mask[:, bass.ds(b * T, T)].unsqueeze(2).broadcast_to([P, T, C])

            link(nc.vector.tensor_reduce(d[:, 0:1], mask[:, :], AX.X, ALU.add))
            dve.wait_ge(f_in, 32)
            for b in range(B):
                link(nc.vector.tensor_tensor(graph_tiles(sqf, b), graph_tiles(yf, b), graph_mask(b), ALU.mult), False)
            mu = ht[:, 0:C]
            dve.wait_ge(f_pe, 1)
            link(nc.vector.reciprocal(d[:, 1:2], turn[:, 0, 0:1]))
            dve.wait_ge(f_pe, 2)
            link(nc.vector.tensor_reduce(ht[:, C:2 * C], acc[:, 0, :].rearrange("p (t c) -> p c t", c=C), AX.X, ALU.add))
            link(nc.vector.tensor_scalar(mu, ht[:, C:2 * C], d[:, 1:2], -1.0, ALU.mult, ALU.mult))
            for b in range(B):
                link(nc.vector.tensor_tensor(graph_tiles(yf, b), graph_tiles(yf, b), over_tiles(mu, T, C), ALU.add))
                link(nc.vector.tensor_tensor(graph(sqf, b), graph(yf, b), graph(yf, b), ALU.mult))
                link(nc.vector.tensor_tensor(graph_tiles(sqf, b), graph_tiles(sqf, b), graph_mask(b), ALU.mult), False)
            dve.wait_ge(f_pe, 3)
            link(nc.vector.tensor_reduce(ht[:, C:2 * C], acc[:, 1, :].rearrange("p (t c) -> p c t", c=C), AX.X, ALU.add))
            link(nc.vector.tensor_scalar(ht[:, 2 * C:3 * C], ht[:, C:2 * C], d[:, 1:2], BN_EPS, ALU.mult, ALU.add))
            dve.wait_ge(f_pool, 1)
            link(nc.vector.tensor_tensor(ht[:, 4 * C:5 * C], ht[:, 3 * C:4 * C], cbias[:, 3, :], ALU.mult))
            scale = ht[:, 4 * C:5 * C]
            for b in range(B):
                m = mean[:, :]
                r = rstd[:, 0, :]
                link(nc.vector.tensor_tensor(graph_tiles(yf, b), graph_tiles(yf, b), over_tiles(scale, T, C), ALU.mult))
                link(nc.vector.tensor_tensor(graph_tiles(yf, b), graph_tiles(yf, b), over_tiles(cbias[:, 4, :], T, C), ALU.add))
                link(nc.vector.tensor_tensor(graph_tiles(yf, b), graph_tiles(yf, b), graph_mask(b), ALU.mult))
                link(nc.vector.scalar_tensor_tensor(graph(xf, b), graph(yf, b), 0.0, graph(xf, b), ALU.max, ALU.add))
                link(nc.vector.tensor_reduce(m, graph_tiles(xf, b), AX.X, ALU.add))
                link(nc.vector.tensor_scalar(m, m, -1.0 / C, None, ALU.mult))
                link(nc.vector.tensor_tensor(graph_tiles(xf, b), graph_tiles(xf, b), m.unsqueeze(2).broadcast_to([P, T, C]), ALU.add))
                dve.wait_ge(f_act, b + 1)
                link(nc.vector.tensor_reduce(r, graph_tiles(sqf, b), AX.X, ALU.add))
                link(nc.vector.tensor_scalar(r, r, 1.0 / C, LN_EPS, ALU.mult, ALU.add))
                dve.wait_ge(f_pool, b + 2)
                link(nc.vector.tensor_tensor(graph_tiles(xf, b), graph_tiles(xf, b),
                                             rstd[:, 1, :].unsqueeze(2).broadcast_to([P, T, C]), ALU.mult))

        DEG_STEPS = 3

        @block.gpsimd
        def _(pool):
            def k_low(n, s, q):
                pool.wait_ge(k_hi[q], n + 1)
                cols = slice(q * W, (q + 1) * W)
                nc.gpsimd.tensor_tensor(pair[:, s, 1, cols], kf[:, q % 2, :], pair[:, s, 0, cols], ALU.subtract)\
                  .then_inc(k_lo[q], 1)

            start_at_one(pool, *k_lo)
            pool.wait_ge(u_step, 2)
            with pool.Fori(0, B) as b:
                with pool.Fori(0, TP) as jj:
                    for s in range(2):
                        n = b * T + jj * 2 + s
                        for q in range(Q - 1):
                            k_low(n, s, q)
                        base = n * DEG_STEPS
                        di = d[:, bass.ds(jj * 2 + s, 1)]
                        pool.wait_ge(deg_done, n + 1)
                        nc.gpsimd.tensor_tensor(di, deg[:, s, 1:2], half_neg[:, 0:1], ALU.pow).then_inc(deg_step, 1)
                        pool.wait_ge(deg_step, base + 1)
                        if s == 0:
                            pool.wait_ge(x_in_done, (b + 1) * 16)
                        pool.wait_ge(slot_used[s], b * T + jj + OPEN)
                        nc.gpsimd.tensor_tensor(vf[:, s, :], x[:, bass.ds((jj * 2 + s) * C, C)],
                                                di.broadcast_to([P, C]), ALU.mult).then_inc(deg_step, 1)
                        pool.wait_ge(deg_step, base + 2)
                        nc.gpsimd.tensor_tensor(vs[:, s, 0:C], vf[:, s, :], ones[:, 0:C], ALU.mult).then_inc(deg_step, 1)
                        pool.wait_ge(deg_step, base + 3)
                        nc.gpsimd.tensor_tensor(vs[:, s, C:P], vf[:, s, :], vs[:, s, 0:C], ALU.subtract).then_inc(v_done, 1)
                        k_low(n, s, Q - 1)
                for e in range(EPI):
                    for h in range(2):
                        r = slice(h * HALF, (h + 1) * HALF)
                        pool.wait_ge(e_veps, b * 2 * EPI + 2 * e + h + 1)
                        nc.gpsimd.tensor_tensor(rstd[:, 1, r], rstd[:, 0, r], half_neg[:, r], ALU.pow).then_inc(e_rstd, 1)
                for h in range(2):
                    r = slice(h * HALF, (h + 1) * HALF)
                    pool.wait_ge(y_floor, b * 2 + h + 1)
                    nc.gpsimd.tensor_tensor(rstd[:, 1, r], rstd[:, 0, r], half_neg[:, r], ALU.pow).then_inc(y_rstd, 1)

            pool.wait_ge(f_dve, FINAL_HEAD - 1)
            nc.gpsimd.tensor_tensor(ht[:, 3 * C:4 * C], ht[:, 2 * C:3 * C], half_neg[:, :], ALU.pow).then_inc(f_pool, 1)
            with pool.Fori(0, B) as b:
                pool.wait_ge(f_dve, FINAL_HEAD + FINAL_STEPS * b + 9)
                nc.gpsimd.tensor_tensor(rstd[:, 1, :], rstd[:, 0, :], half_neg[:, 0:T], ALU.pow).then_inc(f_pool, 1)


def kernel(x, adj, nodemask, L0_gnn_U, L0_gnn_w_scale, L1_gnn_W0, L1_gnn_b0, L1_gnn_W1, L1_gnn_b1, L1_gnn_W2,
           L1_gnn_b2, L1_gnn_Wout, L1_gnn_bout, L2_gnn_weight, L2_gnn_bias, L3_gnn_weight, L3_gnn_bias,
           L3_gnn_gamma, L3_gnn_beta):
    import numpy as np
    import concourse.bacc as bacc
    from concourse.bass_utils import run_bass_kernel_spmd

    products = [(0, 0), (0, 1), (1, 0), (1, 1), (0, 2), (2, 0), (1, 2), (2, 1)]
    pick = np.zeros((P, 6), np.float32)
    for g, (a, c) in enumerate(products):
        pick[g * R:(g + 1) * R, a] = 1.0
        pick[g * R:(g + 1) * R, 3 + c] = 1.0
    eye = np.eye(P, dtype=np.float32)
    fold = np.concatenate([np.eye(C, dtype=np.float32)] * 2)

    def a(v):
        return np.ascontiguousarray(np.asarray(v))

    arrays = {
        "x_in": a(np.asarray(x).reshape(B, T, P, C).transpose(0, 2, 1, 3)).reshape(B, P, NC_),
        "adj": a(adj),
        "mask_in": a(np.asarray(nodemask).reshape(B, T, P).transpose(2, 0, 1)).reshape(P, B * T),
        "ut": a(np.asarray(L0_gnn_U).T),
        "wscale": a(L0_gnn_w_scale).reshape(1),
        "w0": a(L1_gnn_W0), "w1": a(L1_gnn_W1), "w2": a(L1_gnn_W2), "wout": a(L1_gnn_Wout),
        "l2w": a(L2_gnn_weight), "l3w": a(L3_gnn_weight),
        "b0": a(L1_gnn_b0), "b1": a(L1_gnn_b1), "b2": a(L1_gnn_b2), "bout": a(L1_gnn_bout),
        "l2b": a(L2_gnn_bias), "l3b": a(L3_gnn_bias), "gamma": a(L3_gnn_gamma), "beta": a(L3_gnn_beta),
        "ident_in": eye, "fold_in": fold, "pick_in": pick,
    }
    nc = bacc.Bacc("TRN2", target_bir_lowering=False, num_devices=1)
    args = {n: nc.dram_tensor(n, v.shape, mybir.dt.from_np(v.dtype), kind="ExternalInput").ap()
            for n, v in arrays.items()}
    out = nc.dram_tensor("out", (B, P, NC_), F32, kind="ExternalOutput").ap()
    build(nc, *args.values(), out)
    r = run_bass_kernel_spmd(nc, [arrays], core_ids=[0])
    got = r.results[0]["out"]
    return got.reshape(B, P, T, C).transpose(0, 2, 1, 3).reshape(B, N, C)
```

```python
import concourse.bass as bass
from concourse import mybir
from contextlib import ExitStack

F32 = mybir.dt.float32
F16 = mybir.dt.float16
BF16 = mybir.dt.bfloat16
ALU = mybir.AluOpType
ACT = mybir.ActivationFunctionType
AX = mybir.AxisListType

P = 128
B, N, C, H = 8, 2048, 64, 128
T = N // P
TP = T // 2
W = 512
HALF = T // 2
Q = N // W
TQ = W // P
R = 16
NC_ = T * C
LAYERS = 3
LN_EPS = 1e-5
DEG_EPS = 1e-12
BN_EPS = 1e-5
NORM_FLOOR = 1e-12


def build(nc, x_in, adj, mask_in, ut, wscale, w0, w1, w2, wout, l2w, l3w, b0, b1, b2, bout, l2b, l3b,
          gamma, beta, ident_in, fold_in, pick_in, out):
    ctx = ExitStack()
    with ctx:
        def sb(name, shape, dt=F32):
            return ctx.enter_context(nc.sbuf_tensor(name, shape, dt))

        def sem(name):
            return ctx.enter_context(nc.semaphore(name))

        def sems(name, n):
            return [sem(f"{name}{i}") for i in range(n)]

        y_all = nc.dram_tensor("y_all", (B, P, NC_), F32).ap()
        x3_all = nc.dram_tensor("x3_all", (B, P, NC_), F32).ap()

        at = sb("at", [P, 2, T, N], F16)
        pair = sb("pair", [P, 2, 2, N], F16)
        col_ring = sb("col_ring", [P, Q, TQ, P])
        row_ring = sb("row_ring", [P, Q, W])
        sym = sb("sym", [P, 2, W])
        gate = sb("gate", [P, 2, W])
        kf = sb("kf", [P, 2, W])
        ht = sb("ht", [P, N])
        x = sb("x", [P, NC_])
        res = sb("res", [P, NC_])
        xs = sb("xs", [P, T, P], F16)
        ytmp = ht[:, 0:NC_]
        ysq = ht[:, NC_:2 * NC_]
        vs = sb("vs", [P, 2, P], F16)
        vf = sb("vf", [P, 2, C])
        ul = sb("ul", [P, N], BF16)
        ur = sb("ur", [P, N], BF16)
        ident = sb("ident", [P, P])
        ident16 = sb("ident16", [P, P], F16)
        fold = sb("fold", [P, C])
        pick = sb("pick", [P, 6])
        w0s = sb("w0s", [P, H])
        w1s = sb("w1s", [H, H])
        w2s = sb("w2s", [H, H])
        wouts = sb("wouts", [H, C])
        l2ws = sb("l2ws", [P, C])
        l3ws = sb("l3ws", [P, C])
        bias = sb("bias", [P, 2, H])
        cbias = sb("cbias", [P, 5, C])
        mask = sb("mask", [P, B * T])
        wsc = sb("wsc", [P, 1])
        ones = sb("ones", [P, C])
        part = sb("part", [P, 2, Q])
        deg = sb("deg", [P, 2, 2])
        half_neg = sb("half_neg", [P, HALF])
        d = sb("d", [P, T])
        wd = sb("wd", [P, T])
        mean = sb("mean", [P, T])
        rstd = sb("rstd", [P, 2, T])
        w0row = kf[:, 0, 0:H]
        tmp = kf[:, :, :].rearrange("p a w -> p (a w)")
        sq = sym[:, :, :].rearrange("p a w -> p (a w)")

        acc = ctx.enter_context(nc.psum_tensor("acc", [P, Q, W], F32))
        side = ctx.enter_context(nc.psum_tensor("side", [P, 2, 2, W], F32))
        turn, uu = side[:, :, 0, :], side[:, :, 1, :]

        consts_in = sem("consts_in")
        const_made = sem("const_made")
        b0_in = sem("b0_in")
        u_step = sem("u_step")
        col_in = sems("col_in", Q)
        row_in = sems("row_in", Q)
        x_in_done = sem("x_in_done")
        turned = sems("turned", Q)
        uu_done = sems("uu_done", Q)
        at_hi = sems("at_hi", Q)
        at_lo = sems("at_lo", Q)
        row_used = sems("row_used", Q)
        gated = sems("gated", Q)
        k_done = sems("k_done", Q)
        k_hi = sems("k_hi", Q)
        k_lo = sems("k_lo", Q)
        row_hi = sems("row_hi", Q)
        row_lo = sems("row_lo", Q)
        deg_sum = sem("deg_sum")
        deg_done = sem("deg_done")
        deg_step = sem("deg_step")
        v_done = sem("v_done")
        slot_used = sems("slot_used", 2)
        at_used = sem("at_used")
        prod = sem("prod")
        evac = sem("evac")
        proj = sem("proj")
        hid_mm = sem("hid_mm")
        msg_mm = sem("msg_mm")
        msg_f = sem("msg_f")
        msg_hi = sem("msg_hi")
        msg_lo = sem("msg_lo")
        agg = sem("agg")
        relu = sem("relu")
        wd_done = sem("wd_done")
        e_scaled = sem("e_scaled")
        e_sum = sem("e_sum")
        res_step = sem("res_step")
        res_done = sem("res_done")
        cent_sum = sem("cent_sum")
        cent_mean = sem("cent_mean")
        cent_x = sem("cent_x")
        e_sq = sem("e_sq")
        e_var = sem("e_var")
        e_veps = sem("e_veps")
        e_rstd = sem("e_rstd")
        e_x = sem("e_x")
        x_hi = sem("x_hi")
        x_lo = sem("x_lo")
        y_bias = sem("y_bias")
        y_sq = sem("y_sq")
        y_var = sem("y_var")
        y_floor = sem("y_floor")
        y_rstd = sem("y_rstd")
        y_done = sem("y_done")
        y_out = sem("y_out")
        x3_out = sem("x3_out")
        fy_in = sems("fy_in", B)
        fx_in = sems("fx_in", B)
        f_dve = sem("f_dve")
        f_act = sem("f_act")
        f_pe = sem("f_pe")
        f_pool = sem("f_pool")
        f_out = sem("f_out")

        csum = part[:, 0, :]
        all_ones = w2s
        EPI = 3
        HC = HALF * C

        def half(ap, h):
            return ap[:, h * HC:(h + 1) * HC]

        def tiles(ap, h):
            return half(ap, h).rearrange("p (t c) -> p t c", c=C)

        def spread(ap, h):
            return ap[:, h * HALF:(h + 1) * HALF].unsqueeze(2).broadcast_to([P, HALF, C])

        def over_tiles(ap, n, w):
            return ap.unsqueeze(1).broadcast_to([P, n, w])

        def at_q(part_, i, q):
            return at[:, part_, bass.ds(i, 1), q * W:(q + 1) * W].rearrange("p a w -> p (a w)")

        def natural(e, h):
            bank = acc[:, h, :] if e == 3 else turn[:, h, :]
            return bank.rearrange("p (t c) -> p t c", c=C)

        def ring_block(s, q):
            return row_ring[:, q, :] if s == 0 else col_ring[:, q, :, :].rearrange("p t c -> p (t c)")

        PRODS = 3 + 3 + 4

        N_CONSTS = 1 + P // R + 6 + 6 + 2 + 5 + 1 + 1
        W0_STEP = 14
        U_STEPS = W0_STEP + 3 * 4
        FINAL_MU = 1 + B + 3
        FINAL_HEAD = FINAL_MU + 3 * B + 3
        FINAL_STEPS = 10

        OPEN = 1

        def start_at_one(eng, *opened):
            for s in opened:
                eng.sem_inc(s, OPEN)

        block = ctx.enter_context(nc.Block())

        @block.sync
        def _(sp):
            def blocks(b, i, col_free, row_free):
                for q in range(Q):
                    for free, count in col_free:
                        sp.wait_ge(free[q], count)
                    sp.dma_start(col_ring[:, q, :, :],
                                 adj[bass.ds(b, 1), q * W:(q + 1) * W, bass.ds(i * P, P)]
                                 .rearrange("a (t p) c -> p (a t) c", p=P)).then_inc(col_in[q], 16)
                    for free, count in row_free:
                        sp.wait_ge(free[q], count)
                    sp.dma_start(row_ring[:, q, :], row_block(b, i, q)).then_inc(row_in[q], 16)

            def row_block(b, i, q):
                return adj[bass.ds(b, 1), bass.ds(i * P, P), q * W:(q + 1) * W].rearrange("a p c -> p (a c)")

            with sp.Fori(0, B) as b:
                last = [(row_lo, b * T + OPEN)]
                blocks(b, 0, last, last)
                sp.wait_ge(x3_out, (b + 1) * 16)
                sp.wait_ge(x_lo, b * 6 + OPEN)
                sp.dma_start(x[:, :], x_in[bass.ds(b, 1), :, :].rearrange("a p n -> p (a n)")).then_inc(x_in_done, 16)
                with sp.Fori(1, T) as i:
                    blocks(b, i, [(turned, b * T + i + OPEN)], [(row_used, b * T + i + OPEN)])
                for s in range(2):
                    for q in range(Q):
                        sp.wait_ge((row_used if s == 0 else turned)[q], (b + 1) * T + OPEN)
                        sp.dma_start(ring_block(s, q), row_block(b, s, q)).then_inc((row_in if s == 0 else col_in)[q], 16)
                with sp.Fori(1, TP) as jj:
                    for s in range(2):
                        for q in range(Q):
                            sp.wait_ge(row_lo[q], b * T + jj * 2 + s - 1 + OPEN)
                            sp.dma_start(ring_block(s, q), row_block(b, jj * 2 + s, q))\
                              .then_inc((row_in if s == 0 else col_in)[q], 16)
            yf = at[:, 0, 0:8, :].rearrange("p a n -> p (a n)").bitcast(F32)
            xf = at[:, 0, 8:16, :].rearrange("p a n -> p (a n)").bitcast(F32)
            sp.wait_ge(y_out, 16 * (B + 1))
            sp.wait_ge(x3_out, 16 * (B + 1))
            sp.wait_ge(at_used, B * T + T)
            for b in range(B):
                sp.dma_start(yf[:, b * NC_:(b + 1) * NC_], y_all[b]).then_inc(fy_in[b], 16)
            for b in range(B):
                sp.dma_start(xf[:, b * NC_:(b + 1) * NC_], x3_all[b]).then_inc(fx_in[b], 16)
            for b in range(B):
                sp.wait_ge(f_dve, FINAL_HEAD + FINAL_STEPS * (b + 1))
                sp.dma_start(out[b], xf[:, b * NC_:(b + 1) * NC_]).then_inc(f_out, 16)
            sp.wait_ge(f_out, 16 * B)


        @block.tensor
        def _(pe):
            def stripe_units(b, i):
                n = b * T + i
                for q in range(Q):
                    pe.wait_ge(col_in[q], (b * (T + TP) + i + 1) * 16)
                    before, more = (q + 2) % Q, int(q >= 2)
                    pe.wait_ge(at_lo[before], n + more + OPEN)
                    for t in range(TQ):
                        mm = nc.tensor.transpose(turn[:, q % 2, t * P:(t + 1) * P], col_ring[:, q, t, :], ident[:, :])
                    mm.then_inc(turned[q], 1)
                    pe.wait_ge(gated[before], n + more + OPEN)
                    nc.tensor.matmul(uu[:, q % 2, :], ul[:, bass.ds(i * P, P)], ur[:, q * W:(q + 1) * W],
                                     start=True, stop=True).then_inc(uu_done[q], 1)

            def k_product(n, s, first=False, last=False):
                pe.wait_ge(v_done, n + 1)
                for q in range(Q):
                    pe.wait_ge(k_lo[q], n + 1 + OPEN)
                    for h in range(2):
                        mm = nc.tensor.matmul(acc[:, q, :], vs[:, s, :], pair[:, s, h, q * W:(q + 1) * W],
                                              start=(first and h == 0), stop=(last and h == 1))
                    if last and q < Q - 1:
                        mm.then_inc(prod, 1)
                mm.then_inc(slot_used[s], 1)

            def project(e, weights, c):
                for t in range(c * TQ, (c + 1) * TQ):
                    mm = nc.tensor.matmul(natural(e, t // HALF)[:, t % HALF, :], ht[:, t * P:(t + 1) * P],
                                          weights, start=True, stop=True)
                if c % 2:
                    mm.then_inc(proj, 1)

            def project_all(e, b, weights):
                for c in range(Q):
                    pe.wait_ge(evac, (b * 4 + e) * Q + (Q if e == 3 else c + 1))
                    project(e, weights, c)

            def hidden(b, c):
                pe.wait_ge(evac, (b * 4 + 1) * Q + c + 1)
                nc.tensor.matmul(uu[:, c % 2, :], w0s[:, :], ht[:, c * W:(c + 1) * W], start=True, stop=True)\
                  .then_inc(hid_mm, 1)

            def messages(b, k, c):
                pe.wait_ge(relu, (b * LAYERS + k - 1) * Q + c + 1)
                n = (b * 2 + k - 1) * Q + c
                if k > 1 or c >= 2:
                    pe.wait_ge(msg_f, n - 1)
                for t in range(TQ):
                    a = (c * TQ + t) * P
                    mm = nc.tensor.matmul(turn[:, c % 2, t * H:(t + 1) * H], ht[:, a:a + P], (w1s, w2s)[k - 1][:, :],
                                          start=True, stop=True)
                mm.then_inc(msg_mm, 1)

            def agg_step(b, k, c, j, start=False, stop=False):
                s = k - 1
                hi = pair[:, s, 0, bass.ds(j * P, P)]
                lo = pair[:, s, 1, bass.ds(j * P, P)]
                nc.tensor.matmul(acc[:, c, :], hi, at_q(0, j, c), start=start, stop=False)
                nc.tensor.matmul(acc[:, c, :], hi, at_q(1, j, c), start=False, stop=False)
                return nc.tensor.matmul(acc[:, c, :], lo, at_q(0, j, c), start=False, stop=stop)

            def aggregate(b, k, c):
                agg_step(b, k, c, 0, start=True)
                with pe.Fori(1, T - 1, 2) as j:
                    agg_step(b, k, c, j)
                    agg_step(b, k, c, j + 1)
                agg_step(b, k, c, T - 1, stop=True).then_inc(agg, 1)

            def aggregate_tiles(b, k, c, g):
                for j in range(g * TQ, (g + 1) * TQ):
                    mm = agg_step(b, k, c, j, start=(j == 0), stop=(j == T - 1))
                if g == Q - 1:
                    mm.then_inc(agg, 1)

            def first_aggregates(b, k, between):
                for g in range(Q - 1):
                    pe.wait_ge(msg_lo, (b * 2 + k - 1) * Q + g + 1)
                    aggregate_tiles(b, k, 0, g)
                    for step in between[g]:
                        step()
                for g in range(Q - 1):
                    aggregate_tiles(b, k, 1, g)
                pe.wait_ge(msg_lo, (b * 2 + k) * Q)
                for c in range(2):
                    aggregate_tiles(b, k, c, Q - 1)

            def x_step(i, c, h, start=False, stop=False):
                xi = xs[:, bass.ds(i, 1), :].rearrange("p a c -> p (a c)")
                return nc.tensor.matmul(acc[:, c, :], xi, at_q(h, i, c), start=start, stop=stop)

            def x_aggregate(b, c):
                x_step(0, c, 0, start=True)
                x_step(0, c, 1)
                with pe.Fori(1, HALF) as i:
                    x_step(i, c, 0)
                    x_step(i, c, 1)
                if c == 0:
                    pe.wait_ge(x_lo, b * 6 + 2 + OPEN)
                x_step(HALF, c, 0)
                x_step(HALF, c, 1)
                with pe.Fori(HALF + 1, T - 1) as i:
                    x_step(i, c, 0)
                    x_step(i, c, 1)
                x_step(T - 1, c, 0)
                x_step(T - 1, c, 1, stop=True).then_inc(agg, 1)

            def row_product(b, i, s, first=False, last=False):
                for q in range(Q):
                    pe.wait_ge(row_lo[q], b * T + i + 1 + OPEN)
                    for h in range(2):
                        mm = nc.tensor.matmul(acc[:, q, :], xs[:, bass.ds(i, 1), :].rearrange("p a c -> p (a c)"),
                                              pair[:, s, h, q * W:(q + 1) * W],
                                              start=(first and h == 0), stop=(last and h == 1))
                    if last and q < Q - 1:
                        mm.then_inc(prod, 1)
                mm.then_inc(slot_used[s], 1)

            def at_product(i, first=False):
                for q in range(Q):
                    x_step(i, q, 0, start=first)
                    mm = x_step(i, q, 1)
                mm.then_inc(at_used, 1)

            def at_products(lo, hi):
                with pe.Fori(lo, hi) as i:
                    at_product(i)

            def layer_3(b, more):
                pe.wait_ge(x_lo, b * 6 + 5 + OPEN)
                at_product(0, first=True)
                at_products(1, 4)
                if more:
                    stripe_units(b + 1, 0)
                at_products(4, 8)
                pe.wait_ge(x_lo, b * 6 + 6 + OPEN)
                at_product(8)
                if more:
                    stripe_units(b + 1, 1)
                at_products(9, T)
                for t in range(T):
                    mm = nc.tensor.matmul(acc[:, t // TQ, t % TQ * P:(t % TQ + 1) * P], xs[:, t, :], ident16[:, :],
                                          start=False, stop=(t % TQ == TQ - 1))
                    if t % TQ == TQ - 1:
                        mm.then_inc(prod, 1)
                project_all(3, b, l3ws[:, :])
                if more:
                    pe.wait_ge(y_bias, (b + 1) * 2 + OPEN)

            def layers_0_to_2(b):
                k_product(b * T, 0, first=True)
                with pe.Fori(1, TP) as jj:
                    stripe_units(b, jj * 2)
                    k_product(b * T + jj * 2 - 1, 1)
                    stripe_units(b, jj * 2 + 1)
                    k_product(b * T + jj * 2, 0)
                k_product(b * T + T - 1, 1, last=True)
                pe.wait_ge(at_lo[3], (b + 1) * T + OPEN)
                project_all(0, b, fold[:, :])
                pe.wait_ge(x_lo, b * 6 + 1 + OPEN)
                pe.wait_ge(gated[3], (b + 1) * T + OPEN)
                x_aggregate(b, 0)
                x_aggregate(b, 1)
                hidden(b, 0)
                x_aggregate(b, 2)
                hidden(b, 1)
                messages(b, 1, 0)
                x_aggregate(b, 3)
                hidden(b, 2)
                messages(b, 1, 1)
                first_aggregates(b, 1, [[lambda: hidden(b, 3), lambda: messages(b, 1, 2)],
                                        [lambda: messages(b, 1, 3)], []])
                aggregate(b, 1, 2)
                messages(b, 2, 0)
                messages(b, 2, 1)
                aggregate(b, 1, 3)
                messages(b, 2, 2)
                first_aggregates(b, 2, [[lambda: messages(b, 2, 3)], [], []])
                aggregate(b, 2, 2)
                pe.wait_ge(msg_f, (b + 1) * 2 * Q)
                for c in range(Q):
                    if c == 2:
                        aggregate(b, 2, 3)
                    pe.wait_ge(relu, (b * LAYERS + 2) * Q + c + 1)
                    project(1, wouts[:, :], c)
                pe.wait_ge(x_lo, b * 6 + 3 + OPEN)
                row_product(b, 0, 0, first=True)
                row_product(b, 1, 1)
                with pe.Fori(1, TP // 2) as jj:
                    row_product(b, jj * 2, 0)
                    row_product(b, jj * 2 + 1, 1)
                pe.wait_ge(x_lo, b * 6 + 4 + OPEN)
                row_product(b, HALF, 0)
                row_product(b, HALF + 1, 1)
                with pe.Fori(TP // 2 + 1, TP - 1) as jj:
                    row_product(b, jj * 2, 0)
                    row_product(b, jj * 2 + 1, 1)
                row_product(b, T - 2, 0)
                row_product(b, T - 1, 1, last=True)
                project_all(2, b, l2ws[:, :])

            start_at_one(pe, *turned, *slot_used)
            pe.sem_inc(at_used, T)
            pe.wait_ge(u_step, W0_STEP - 1)
            pe.wait_ge(const_made, 1)
            stripe_units(0, 0)
            stripe_units(0, 1)
            pe.wait_ge(b0_in, 32)
            pe.wait_ge(u_step, U_STEPS)
            with pe.Fori(0, B - 1) as b:
                layers_0_to_2(b)
                layer_3(b, True)
            layers_0_to_2(B - 1)
            layer_3(B - 1, False)

            yf = at[:, 0, 0:8, :].rearrange("p a n -> p (a n)").bitcast(F32)
            sqf = at[:, 1, 0:8, :].rearrange("p a n -> p (a n)").bitcast(F32)
            pe.wait_ge(f_dve, 1)
            pe.wait_ge(const_made, 2)
            nc.tensor.matmul(turn[:, 0, 0:1], all_ones[:, :], d[:, 0:1], start=True, stop=True).then_inc(f_pe, 1)
            for b in range(B):
                pe.wait_ge(f_dve, 2 + b)
                for h in range(2):
                    a = (2 * b + h) * HC
                    mm = nc.tensor.matmul(acc[:, 0, :], all_ones[:, :], sqf[:, a:a + HC], start=(a == 0),
                                          stop=(a == (2 * B - 1) * HC))
            mm.then_inc(f_pe, 1)
            for b in range(B):
                pe.wait_ge(f_dve, FINAL_MU + 3 * (b + 1))
                for h in range(2):
                    a = (2 * b + h) * HC
                    mm = nc.tensor.matmul(acc[:, 1, :], all_ones[:, :], sqf[:, a:a + HC], start=(a == 0),
                                          stop=(a == (2 * B - 1) * HC))
            mm.then_inc(f_pe, 1)

        @block.scalar
        def _(act):
            def head(b, i, q):
                n = b * T + i
                act.wait_ge(turned[q], n + 1 + OPEN)
                if q == 0:
                    act.wait_ge(at_used, n + 1)
                nc.scalar.activation(at_q(0, i, q), turn[:, q % 2, :], ACT.Copy).then_inc(at_hi[q], 1)
                act.wait_ge(uu_done[q], n + 1)
                act.wait_ge(k_done[(q + 2) % Q], n + int(q >= 2) + OPEN)
                nc.scalar.activation(gate[:, q % 2, :], uu[:, q % 2, :], ACT.Sigmoid).then_inc(gated[q], 1)

            def k_high(b, jj, n, s, q):
                act.wait_ge(k_done[q], n + 1 + OPEN)
                if q == 0:
                    act.wait_ge(slot_used[s], b * T + jj + OPEN)
                nc.scalar.activation(pair[:, s, 0, q * W:(q + 1) * W], kf[:, q % 2, :], ACT.Copy).then_inc(k_hi[q], 1)

            def pair_of_stripes(b, jj, last):
                for k in range(2 * Q):
                    nk = k + 1
                    if nk < 2 * Q:
                        head(b, jj * 2 + nk // Q, nk % Q)
                    elif not last:
                        head(b, jj * 2 + 2, 0)
                    k_high(b, jj, b * T + jj * 2 + k // Q, k // Q, k % Q)

            def norm_steps(b, e):
                for h in range(2):
                    act.wait_ge(e_sum, b * 2 * EPI + 2 * e + h + 1)
                    nc.scalar.activation(half(sq, h), half(tmp, h), ACT.Square).then_inc(e_sq, 1)

            def x_high(b, e):
                keep = C - 1 if e == 0 else C
                for h in range(2):
                    act.wait_ge(e_x, b * 2 * EPI + 2 * e + h + 1)
                    nc.scalar.activation(xs[:, h * HALF:(h + 1) * HALF, 0:keep], tiles(x, h)[:, :, 0:keep], ACT.Copy)\
                      .then_inc(x_hi, 1)

            def evacuate(b, e, c):
                if e == 0:
                    if c == 0:
                        act.wait_ge(y_out, (b + 1) * 16)
                    if c < Q - 1:
                        act.wait_ge(prod, b * PRODS + c + 1)
                    else:
                        act.wait_ge(slot_used[1], b * T + TP + OPEN)
                elif e == 1:
                    act.wait_ge(agg, b * LAYERS * Q + c + 1)
                elif e == 2:
                    if c < Q - 1:
                        act.wait_ge(prod, b * PRODS + 3 + c + 1)
                    else:
                        act.wait_ge(slot_used[1], (b + 1) * T + OPEN)
                else:
                    act.wait_ge(prod, b * PRODS + 6 + c + 1)
                nc.scalar.activation(ht[:, c * W:(c + 1) * W], acc[:, c, :], ACT.Copy).then_inc(evac, 1)

            def rectify(b, k, c):
                if k == 0:
                    act.wait_ge(hid_mm, b * Q + c + 1)
                else:
                    act.wait_ge(agg, (b * LAYERS + k) * Q + c + 1)
                nc.scalar.activation(ht[:, c * W:(c + 1) * W], uu[:, c % 2, :] if k == 0 else acc[:, c, :],
                                     ACT.Relu).then_inc(relu, 1)

            def message_high(b, k, c):
                act.wait_ge(msg_f, (b * 2 + k - 1) * Q + c + 1)
                if c == 0:
                    act.wait_ge(slot_used[k - 1], b * T + TP + OPEN)
                nc.scalar.activation(pair[:, k - 1, 0, c * W:(c + 1) * W], kf[:, c % 2, :], ACT.Copy).then_inc(msg_hi, 1)

            def row_high(b, jj, s, q):
                act.wait_ge((row_in if s == 0 else col_in)[q], (b * (T + TP) + T + jj + 1) * 16)
                if q == 0:
                    act.wait_ge(agg, (b * LAYERS + 2 + s) * Q)
                    act.wait_ge(slot_used[s], b * T + TP + jj + OPEN)
                nc.scalar.activation(pair[:, s, 0, q * W:(q + 1) * W], ring_block(s, q), ACT.Copy).then_inc(row_hi[q], 1)

            def layers_0_to_2(b):
                head(b, 2, 0)
                with act.Fori(1, TP - 1) as jj:
                    pair_of_stripes(b, jj, False)
                pair_of_stripes(b, TP - 1, True)
                for c in range(Q):
                    evacuate(b, 0, c)
                norm_steps(b, 0)
                x_high(b, 0)
                evacuate(b, 1, 0)
                evacuate(b, 1, 1)
                rectify(b, 0, 0)
                evacuate(b, 1, 2)
                rectify(b, 0, 1)
                message_high(b, 1, 0)
                evacuate(b, 1, 3)
                rectify(b, 0, 2)
                message_high(b, 1, 1)
                rectify(b, 0, 3)
                message_high(b, 1, 2)
                message_high(b, 1, 3)
                rectify(b, 1, 0)
                rectify(b, 1, 1)
                rectify(b, 1, 2)
                message_high(b, 2, 0)
                message_high(b, 2, 1)
                rectify(b, 1, 3)
                message_high(b, 2, 2)
                message_high(b, 2, 3)
                for q in range(Q):
                    row_high(b, 0, 0, q)
                for c in range(Q):
                    rectify(b, 2, c)
                norm_steps(b, 1)
                x_high(b, 1)
                for q in range(Q):
                    row_high(b, 0, 1, q)
                with act.Fori(1, TP) as jj:
                    for s in range(2):
                        for q in range(Q):
                            row_high(b, jj, s, q)
                for c in range(Q):
                    evacuate(b, 2, c)
                norm_steps(b, 2)
                x_high(b, 2)
                act.dma_start(x3_all[bass.ds(b, 1), :, :].rearrange("a p n -> p (a n)"), x[:, :]).then_inc(x3_out, 16)

            def layer_3(b, more):
                if more:
                    head(b + 1, 0, 0)
                    pair_of_stripes(b + 1, 0, True)
                for c in range(Q):
                    evacuate(b, 3, c)
                act.wait_ge(proj, (b + 1) * 8)
                for h in range(2):
                    act.wait_ge(y_bias, b * 2 + h + 1 + OPEN)
                    nc.scalar.activation(half(ysq, h), half(ytmp, h), ACT.Square).then_inc(y_sq, 1)
                act.wait_ge(y_done, b * 2 + 2)
                act.dma_start(y_all[bass.ds(b, 1), :, :].rearrange("a p n -> p (a n)"), ytmp).then_inc(y_out, 16)

            start_at_one(act, *gated)
            act.sem_inc(x3_out, 16)
            act.sem_inc(y_out, 16)
            act.dma_start(pick[:, :], pick_in).then_inc(consts_in, 16)
            for g in range(P // R):
                act.dma_start(ht[g * R:(g + 1) * R, :], ut).then_inc(consts_in, 16)
            for dst, src in ((ident, ident_in), (fold, fold_in), (w1s, w1), (w2s, w2), (wouts, wout), (mask, mask_in)):
                act.dma_start(dst[:, :], src).then_inc(consts_in, 16)
            for h in range(2):
                act.dma_start(w0s[h * C:(h + 1) * C, :], w0).then_inc(consts_in, 16)
                act.dma_start(l2ws[h * C:(h + 1) * C, :], l2w).then_inc(consts_in, 16)
                act.dma_start(l3ws[h * C:(h + 1) * C, :], l3w).then_inc(consts_in, 16)
            for n, v in enumerate((b1, b2)):
                act.dma_start(bias[:, n, :], v.partition_broadcast(P)).then_inc(consts_in, 16)
            for n, v in enumerate((bout, l2b, l3b, gamma, beta)):
                act.dma_start(cbias[:, n, :], v.partition_broadcast(P)).then_inc(consts_in, 16)
            act.dma_start(wsc[:, :], wscale.partition_broadcast(P)).then_inc(consts_in, 16)
            act.dma_start(w0row, w0[C - 1, :].partition_broadcast(P)).then_inc(consts_in, 16)
            act.wait_ge(consts_in, N_CONSTS * 16)
            nc.scalar.activation(ident16[:, :], ident[:, :], ACT.Copy).then_inc(const_made, 1)
            head(0, 0, 0)
            pair_of_stripes(0, 0, True)
            act.wait_ge(u_step, W0_STEP)
            for h in range(2):
                act.dma_start(w0s[(h + 1) * C - 1:(h + 1) * C, :], b0.rearrange("(a h) -> a h", a=1)).then_inc(b0_in, 16)
            with act.Fori(0, B - 1) as b:
                layers_0_to_2(b)
                layer_3(b, True)
            layers_0_to_2(B - 1)
            layer_3(B - 1, False)
            xf = at[:, 0, 8:16, :].rearrange("p a n -> p (a n)").bitcast(F32)
            sqf = at[:, 1, 0:8, :].rearrange("p a n -> p (a n)").bitcast(F32)
            with act.Fori(0, B) as b:
                act.wait_ge(f_dve, FINAL_HEAD + FINAL_STEPS * b + 7)
                nc.scalar.activation(sqf[:, bass.ds(b * NC_, NC_)], xf[:, bass.ds(b * NC_, NC_)], ACT.Square)\
                  .then_inc(f_act, 1)

        @block.vector
        def _(dve):
            def unit(b, jj, s, q):
                i = jj * 2 + s
                n = b * T + i
                dve.wait_ge(row_in[q], (b * (T + TP) + i + 1) * 16)
                dve.wait_ge(at_hi[q], n + 1)
                nc.vector.tensor_tensor(sym[:, q % 2, :], row_ring[:, q, :], turn[:, q % 2, :], ALU.add)\
                  .then_inc(row_used[q], 1)
                nc.vector.tensor_tensor(at_q(1, i, q), turn[:, q % 2, :], at_q(0, i, q), ALU.subtract)\
                  .then_inc(at_lo[q], 1)
                dve.wait_ge(row_used[q], n + 1 + OPEN)
                dve.wait_ge(gated[q], n + 1 + OPEN)
                dve.wait_ge(k_lo[(q + 2) % Q], n + int(q >= 2) + OPEN)
                nc.vector.scalar_tensor_tensor(kf[:, q % 2, :], sym[:, q % 2, :], 1.0, gate[:, q % 2, :], ALU.mult,
                                               ALU.mult, accum_out=part[:, s, q:q + 1]).then_inc(k_done[q], 1)

            def degree(n, s):
                for q in range(Q):
                    dve.wait_ge(k_done[q], n + 1 + OPEN)
                nc.vector.tensor_reduce(deg[:, s, 0:1], part[:, s, :], AX.X, ALU.add).then_inc(deg_sum, 1)
                dve.wait_ge(deg_sum, n + 1)
                nc.vector.tensor_scalar(deg[:, s, 1:2], deg[:, s, 0:1], 0.5, DEG_EPS, ALU.mult, ALU.max)\
                  .then_inc(deg_done, 1)

            def centre_x(b):
                dve.wait_ge(x_in_done, (b + 1) * 16)
                nc.vector.tensor_reduce(mean[:, :], x[:, :].rearrange("p (t c) -> p t c", c=C), AX.X, ALU.add)\
                  .then_inc(cent_sum, 1)
                dve.wait_ge(cent_sum, b + 1)
                nc.vector.tensor_scalar(mean[:, :], mean[:, :], -1.0 / C, None, ALU.mult).then_inc(cent_mean, 1)
                dve.wait_ge(cent_mean, b + 1)
                for h in range(2):
                    ins = nc.vector.tensor_tensor(tiles(res, h), tiles(x, h), spread(mean, h), ALU.add)
                ins.then_inc(cent_x, 1)

            def norm(b, e):
                v = b * 2 * EPI + 2 * e + 1
                for h in range(2):
                    dve.wait_ge(proj, b * 8 + 2 * e + h + 1)
                    if e == 0:
                        nc.vector.tensor_tensor(tiles(tmp, h), natural(e, h), spread(wd, h), ALU.mult).then_inc(e_scaled, 1)
                    elif e == 1:
                        m = mask[:, bass.ds(b * T + h * HALF, HALF)].unsqueeze(2).broadcast_to([P, HALF, C])
                        nc.vector.tensor_tensor(tiles(tmp, h), natural(e, h), m, ALU.mult).then_inc(e_scaled, 1)
                    if e < 2:
                        dve.wait_ge(e_scaled, b * 4 + 2 * e + h + 1)
                    if e == 0:
                        dve.wait_ge(cent_x, b + 1)
                    elif h == 0:
                        dve.wait_ge(res_done, b * 2 + e)
                    nc.vector.tensor_tensor(half(tmp, h), half(tmp, h) if e < 2 else turn[:, h, :], half(res, h),
                                            ALU.add).then_inc(e_sum, 1)
                for h in range(2):
                    r = rstd[:, 0, h * HALF:(h + 1) * HALF]
                    dve.wait_ge(e_sq, v + h)
                    nc.vector.tensor_reduce(r, tiles(sq, h), AX.X, ALU.add).then_inc(e_var, 1)
                    dve.wait_ge(e_var, v + h)
                    nc.vector.tensor_scalar(r, r, 1.0 / C, LN_EPS, ALU.mult, ALU.add).then_inc(e_veps, 1)
                for h in range(2):
                    dve.wait_ge(e_rstd, v + h)
                    nc.vector.tensor_tensor(tiles(x, h), tiles(tmp, h), spread(rstd[:, 1, :], h), ALU.mult).then_inc(e_x, 1)

            def x_low(b, e):
                keep = C - 1 if e == 0 else C
                for h in range(2):
                    dve.wait_ge(x_hi, b * 6 + 2 * e + h + 1)
                    s = slice(h * HALF, (h + 1) * HALF)
                    if e == 0:
                        nc.vector.memset(xs[:, s, C - 1:C], 1.0)
                        nc.vector.memset(xs[:, s, P - 1:P], 0.0)
                    nc.vector.tensor_tensor(xs[:, s, C:C + keep], tiles(x, h)[:, :, 0:keep], xs[:, s, 0:keep],
                                            ALU.subtract).then_inc(x_lo, 1)

            def message(b, k, c):
                n = (b * 2 + k - 1) * Q + c
                dve.wait_ge(msg_mm, n + 1)
                nc.vector.tensor_tensor(kf[:, c % 2, :].rearrange("p (t h) -> p t h", h=H),
                                        turn[:, c % 2, :].rearrange("p (t h) -> p t h", h=H),
                                        over_tiles(bias[:, k - 1, :], TQ, H), ALU.add).then_inc(msg_f, 1)
                dve.wait_ge(msg_f, n + 1)
                dve.wait_ge(msg_hi, n + 1)
                cols = slice(c * W, (c + 1) * W)
                nc.vector.tensor_tensor(pair[:, k - 1, 1, cols], kf[:, c % 2, :], pair[:, k - 1, 0, cols],
                                        ALU.subtract).then_inc(msg_lo, 1)

            def row_low(b, i, s, q):
                dve.wait_ge(row_hi[q], b * T + i + 1)
                cols = slice(q * W, (q + 1) * W)
                nc.vector.tensor_tensor(pair[:, s, 1, cols], ring_block(s, q), pair[:, s, 0, cols], ALU.subtract)\
                  .then_inc(row_lo[q], 1)

            def stripe(b, jj, s):
                for q in range(Q):
                    unit(b, jj, s, q)
                degree(b * T + jj * 2 + s, s)

            def layers_0_to_2(b):
                with dve.Fori(1, TP) as jj:
                    for s in range(2):
                        stripe(b, jj, s)
                dve.wait_ge(v_done, (b + 1) * T)
                nc.vector.tensor_scalar(wd[:, :], d[:, :], wsc[:, :], 0.5, ALU.mult, ALU.mult).then_inc(wd_done, 1)
                dve.wait_ge(wd_done, b + 1)
                norm(b, 0)
                x_low(b, 0)
                for k in range(1, LAYERS):
                    for c in range(Q):
                        message(b, k, c)
                for q in range(Q):
                    row_low(b, 0, 0, q)
                norm(b, 1)
                x_low(b, 1)
                for q in range(Q):
                    row_low(b, 1, 1, q)
                with dve.Fori(1, TP) as jj:
                    for s in range(2):
                        for q in range(Q):
                            row_low(b, jj * 2 + s, s, q)
                norm(b, 2)
                x_low(b, 2)

            def layer_3(b, more):
                if more:
                    centre_x(b + 1)
                    for s in range(2):
                        stripe(b + 1, 0, s)
                for h in range(2):
                    dve.wait_ge(proj, b * 8 + 6 + h + 1)
                    nc.vector.tensor_tensor(tiles(ytmp, h), natural(3, h), over_tiles(cbias[:, 2, :], HALF, C),
                                            ALU.add).then_inc(y_bias, 1)
                for h in range(2):
                    r = rstd[:, 0, h * HALF:(h + 1) * HALF]
                    dve.wait_ge(y_sq, b * 2 + h + 1)
                    nc.vector.tensor_reduce(r, tiles(ysq, h), AX.X, ALU.add).then_inc(y_var, 1)
                    dve.wait_ge(y_var, b * 2 + h + 1)
                    nc.vector.tensor_scalar(r, r, NORM_FLOOR ** 2, None, ALU.max).then_inc(y_floor, 1)
                for h in range(2):
                    dve.wait_ge(y_rstd, b * 2 + h + 1)
                    nc.vector.tensor_tensor(tiles(ytmp, h), tiles(ytmp, h), spread(rstd[:, 1, :], h), ALU.mult)\
                      .then_inc(y_done, 1)

            start_at_one(dve, *row_used, *row_lo, *at_lo, *k_done, x_lo, y_bias)
            u = [0]

            def u_next(ins):
                u[0] += 1
                ins.then_inc(u_step, 1)
                dve.wait_ge(u_step, u[0])

            u_next(nc.vector.memset(ones[:, :], 1.0))
            u_next(nc.vector.memset(half_neg[:, :], -0.5))
            dve.wait_ge(consts_in, N_CONSTS * 16)
            u1 = pair[:, 0, 0, :].bitcast(BF16)
            u_next(nc.vector.tensor_copy(u1, ht[:, :]))
            for lr, dst in ((0, ul), (1, ur)):
                u_next(nc.vector.tensor_scalar(dst[:, :], u1, pick[:, 3 * lr:3 * lr + 1], None, ALU.mult))
            for n in (1, 2):
                u_next(nc.vector.tensor_tensor(ht[:, :], ht[:, :], u1, ALU.subtract))
                u_next(nc.vector.tensor_copy(u1, ht[:, :]))
                for lr, dst in ((0, ul), (1, ur)):
                    u_next(nc.vector.scalar_tensor_tensor(dst[:, :], u1, pick[:, 3 * lr + n:3 * lr + n + 1],
                                                          dst[:, :], ALU.mult, ALU.add))
            u_next(nc.vector.tensor_tensor(w0s[:, :], w0s[:, :], w0row, ALU.subtract))
            for w in (wouts[:, :], l2ws[:, :], cbias[:, 0, :], cbias[:, 1, :]):
                u_next(nc.vector.tensor_reduce(csum[:, 0:1], w, AX.X, ALU.add))
                u_next(nc.vector.tensor_scalar(csum[:, 1:2], csum[:, 0:1], -1.0 / C, None, ALU.mult))
                u_next(nc.vector.tensor_scalar(w, w, csum[:, 1:2], None, ALU.add))
            assert u[0] == U_STEPS

            centre_x(0)
            for s in range(2):
                stripe(0, 0, s)
            with dve.Fori(0, B - 1) as b:
                layers_0_to_2(b)
                layer_3(b, True)
            layers_0_to_2(B - 1)
            layer_3(B - 1, False)

            yf = at[:, 0, 0:8, :].rearrange("p a n -> p (a n)").bitcast(F32)
            xf = at[:, 0, 8:16, :].rearrange("p a n -> p (a n)").bitcast(F32)
            sqf = at[:, 1, 0:8, :].rearrange("p a n -> p (a n)").bitcast(F32)
            step = [0]

            def link(ins, wait=True):
                step[0] += 1
                ins.then_inc(f_dve, 1)
                if wait:
                    dve.wait_ge(f_dve, step[0])

            def graph(ap, b):
                return ap[:, bass.ds(b * NC_, NC_)]

            def graph_tiles(ap, b):
                return graph(ap, b).rearrange("p (t c) -> p t c", c=C)

            def graph_mask(b):
                return mask[:, bass.ds(b * T, T)].unsqueeze(2).broadcast_to([P, T, C])

            nc.vector.memset(all_ones[:, :], 1.0).then_inc(const_made, 1)
            link(nc.vector.tensor_reduce(d[:, 0:1], mask[:, :], AX.X, ALU.add))
            for b in range(B):
                dve.wait_ge(fy_in[b], 16)
                link(nc.vector.tensor_tensor(graph_tiles(sqf, b), graph_tiles(yf, b), graph_mask(b), ALU.mult), False)
            mu = ht[:, 0:C]
            dve.wait_ge(f_pe, 1)
            link(nc.vector.reciprocal(d[:, 1:2], turn[:, 0, 0:1]))
            dve.wait_ge(f_pe, 2)
            link(nc.vector.tensor_reduce(ht[:, C:2 * C], acc[:, 0, :].rearrange("p (t c) -> p c t", c=C), AX.X, ALU.add))
            link(nc.vector.tensor_scalar(mu, ht[:, C:2 * C], d[:, 1:2], -1.0, ALU.mult, ALU.mult))
            for b in range(B):
                link(nc.vector.tensor_tensor(graph_tiles(yf, b), graph_tiles(yf, b), over_tiles(mu, T, C), ALU.add))
                link(nc.vector.tensor_tensor(graph(sqf, b), graph(yf, b), graph(yf, b), ALU.mult))
                link(nc.vector.tensor_tensor(graph_tiles(sqf, b), graph_tiles(sqf, b), graph_mask(b), ALU.mult), False)
            dve.wait_ge(f_pe, 3)
            link(nc.vector.tensor_reduce(ht[:, C:2 * C], acc[:, 1, :].rearrange("p (t c) -> p c t", c=C), AX.X, ALU.add))
            link(nc.vector.tensor_scalar(ht[:, 2 * C:3 * C], ht[:, C:2 * C], d[:, 1:2], BN_EPS, ALU.mult, ALU.add))
            dve.wait_ge(f_pool, 1)
            link(nc.vector.tensor_tensor(ht[:, 4 * C:5 * C], ht[:, 3 * C:4 * C], cbias[:, 3, :], ALU.mult))
            scale = ht[:, 4 * C:5 * C]
            for b in range(B):
                m = mean[:, :]
                r = rstd[:, 0, :]
                link(nc.vector.tensor_tensor(graph_tiles(yf, b), graph_tiles(yf, b), over_tiles(scale, T, C), ALU.mult))
                link(nc.vector.tensor_tensor(graph_tiles(yf, b), graph_tiles(yf, b), over_tiles(cbias[:, 4, :], T, C), ALU.add))
                link(nc.vector.tensor_tensor(graph_tiles(yf, b), graph_tiles(yf, b), graph_mask(b), ALU.mult))
                dve.wait_ge(fx_in[b], 16)
                link(nc.vector.scalar_tensor_tensor(graph(xf, b), graph(yf, b), 0.0, graph(xf, b), ALU.max, ALU.add))
                link(nc.vector.tensor_reduce(m, graph_tiles(xf, b), AX.X, ALU.add))
                link(nc.vector.tensor_scalar(m, m, -1.0 / C, None, ALU.mult))
                link(nc.vector.tensor_tensor(graph_tiles(xf, b), graph_tiles(xf, b), m.unsqueeze(2).broadcast_to([P, T, C]), ALU.add))
                dve.wait_ge(f_act, b + 1)
                link(nc.vector.tensor_reduce(r, graph_tiles(sqf, b), AX.X, ALU.add))
                link(nc.vector.tensor_scalar(r, r, 1.0 / C, LN_EPS, ALU.mult, ALU.add))
                dve.wait_ge(f_pool, b + 2)
                link(nc.vector.tensor_tensor(graph_tiles(xf, b), graph_tiles(xf, b),
                                             rstd[:, 1, :].unsqueeze(2).broadcast_to([P, T, C]), ALU.mult))

        DEG_STEPS = 3

        @block.gpsimd
        def _(pool):
            def k_low(n, s, q):
                pool.wait_ge(k_hi[q], n + 1)
                cols = slice(q * W, (q + 1) * W)
                nc.gpsimd.tensor_tensor(pair[:, s, 1, cols], kf[:, q % 2, :], pair[:, s, 0, cols], ALU.subtract)\
                  .then_inc(k_lo[q], 1)

            start_at_one(pool, *k_lo)
            pool.wait_ge(u_step, 2)
            def stripe(b, jj, s):
                n = b * T + jj * 2 + s
                for q in range(Q - 1):
                    k_low(n, s, q)
                base = n * DEG_STEPS
                di = d[:, bass.ds(jj * 2 + s, 1)]
                pool.wait_ge(deg_done, n + 1)
                nc.gpsimd.tensor_tensor(di, deg[:, s, 1:2], half_neg[:, 0:1], ALU.pow).then_inc(deg_step, 1)
                pool.wait_ge(deg_step, base + 1)
                pool.wait_ge(x_in_done, (b + 1) * 16)
                pool.wait_ge(slot_used[s], b * T + jj + OPEN)
                nc.gpsimd.tensor_tensor(vf[:, s, :], x[:, bass.ds((jj * 2 + s) * C, C)],
                                        di.broadcast_to([P, C]), ALU.mult).then_inc(deg_step, 1)
                pool.wait_ge(deg_step, base + 2)
                nc.gpsimd.tensor_tensor(vs[:, s, 0:C], vf[:, s, :], ones[:, 0:C], ALU.mult).then_inc(deg_step, 1)
                pool.wait_ge(deg_step, base + 3)
                nc.gpsimd.tensor_tensor(vs[:, s, C:P], vf[:, s, :], vs[:, s, 0:C], ALU.subtract).then_inc(v_done, 1)
                k_low(n, s, Q - 1)

            def deviation(b, e):
                for h in range(2):
                    r = slice(h * HALF, (h + 1) * HALF)
                    pool.wait_ge(e_veps, b * 2 * EPI + 2 * e + h + 1)
                    nc.gpsimd.tensor_tensor(rstd[:, 1, r], rstd[:, 0, r], half_neg[:, :], ALU.pow).then_inc(e_rstd, 1)

            def residual(b, e):
                pool.wait_ge(e_x, b * 2 * EPI + 2 * e)
                all_tiles = res[:, :].rearrange("p (t c) -> p t c", c=C)
                bias_e = over_tiles(cbias[:, e - 1, :], T, C)
                if e == 1:
                    m = mask[:, bass.ds(b * T, T)].unsqueeze(2).broadcast_to([P, T, C])
                    nc.gpsimd.tensor_tensor(all_tiles, bias_e, m, ALU.mult).then_inc(res_step, 1)
                    pool.wait_ge(res_step, b + 1)
                    nc.gpsimd.tensor_tensor(res[:, :], res[:, :], x[:, :], ALU.add).then_inc(res_done, 1)
                else:
                    nc.gpsimd.tensor_tensor(all_tiles, x[:, :].rearrange("p (t c) -> p t c", c=C), bias_e,
                                            ALU.add).then_inc(res_done, 1)

            def layers_0_to_2(b):
                with pool.Fori(1, TP) as jj:
                    for s in range(2):
                        stripe(b, jj, s)
                deviation(b, 0)
                residual(b, 1)
                deviation(b, 1)
                residual(b, 2)
                deviation(b, 2)

            def layer_3(b, more):
                if more:
                    for s in range(2):
                        stripe(b + 1, 0, s)
                for h in range(2):
                    r = slice(h * HALF, (h + 1) * HALF)
                    pool.wait_ge(y_floor, b * 2 + h + 1)
                    nc.gpsimd.tensor_tensor(rstd[:, 1, r], rstd[:, 0, r], half_neg[:, :], ALU.pow).then_inc(y_rstd, 1)

            for s in range(2):
                stripe(0, 0, s)
            with pool.Fori(0, B - 1) as b:
                layers_0_to_2(b)
                layer_3(b, True)
            layers_0_to_2(B - 1)
            layer_3(B - 1, False)

            pool.wait_ge(f_dve, FINAL_HEAD - 1)
            nc.gpsimd.tensor_tensor(ht[:, 3 * C:4 * C], ht[:, 2 * C:3 * C], half_neg[:, 0:1].broadcast_to([P, C]), ALU.pow).then_inc(f_pool, 1)
            with pool.Fori(0, B) as b:
                pool.wait_ge(f_dve, FINAL_HEAD + FINAL_STEPS * b + 9)
                nc.gpsimd.tensor_tensor(rstd[:, 1, :], rstd[:, 0, :], half_neg[:, 0:1].broadcast_to([P, T]), ALU.pow).then_inc(f_pool, 1)


def kernel(x, adj, nodemask, L0_gnn_U, L0_gnn_w_scale, L1_gnn_W0, L1_gnn_b0, L1_gnn_W1, L1_gnn_b1, L1_gnn_W2,
           L1_gnn_b2, L1_gnn_Wout, L1_gnn_bout, L2_gnn_weight, L2_gnn_bias, L3_gnn_weight, L3_gnn_bias,
           L3_gnn_gamma, L3_gnn_beta):
    import numpy as np
    import concourse.bacc as bacc
    from concourse.bass_utils import run_bass_kernel_spmd

    products = [(0, 0), (0, 1), (1, 0), (1, 1), (0, 2), (2, 0), (1, 2), (2, 1)]
    pick = np.zeros((P, 6), np.float32)
    for g, (a, c) in enumerate(products):
        pick[g * R:(g + 1) * R, a] = 1.0
        pick[g * R:(g + 1) * R, 3 + c] = 1.0
    eye = np.eye(P, dtype=np.float32)
    fold = np.concatenate([np.eye(C, dtype=np.float32)] * 2) - np.float32(1.0 / C)

    def a(v):
        return np.ascontiguousarray(np.asarray(v))

    arrays = {
        "x_in": a(np.asarray(x).reshape(B, T, P, C).transpose(0, 2, 1, 3)).reshape(B, P, NC_),
        "adj": a(adj),
        "mask_in": a(np.asarray(nodemask).reshape(B, T, P).transpose(2, 0, 1)).reshape(P, B * T),
        "ut": a(np.asarray(L0_gnn_U).T),
        "wscale": a(L0_gnn_w_scale).reshape(1),
        "w0": a(L1_gnn_W0), "w1": a(L1_gnn_W1), "w2": a(L1_gnn_W2), "wout": a(L1_gnn_Wout),
        "l2w": a(L2_gnn_weight), "l3w": a(L3_gnn_weight),
        "b0": a(L1_gnn_b0), "b1": a(L1_gnn_b1), "b2": a(L1_gnn_b2), "bout": a(L1_gnn_bout),
        "l2b": a(L2_gnn_bias), "l3b": a(L3_gnn_bias), "gamma": a(L3_gnn_gamma), "beta": a(L3_gnn_beta),
        "ident_in": eye, "fold_in": fold, "pick_in": pick,
    }
    nc = bacc.Bacc("TRN2", target_bir_lowering=False, num_devices=1)
    args = {n: nc.dram_tensor(n, v.shape, mybir.dt.from_np(v.dtype), kind="ExternalInput").ap()
            for n, v in arrays.items()}
    out = nc.dram_tensor("out", (B, P, NC_), F32, kind="ExternalOutput").ap()
    build(nc, *args.values(), out)
    r = run_bass_kernel_spmd(nc, [arrays], core_ids=[0])
    got = r.results[0]["out"]
    return got.reshape(B, P, T, C).transpose(0, 2, 1, 3).reshape(B, N, C)
```

```python
import concourse.bass as bass
from concourse import mybir
from contextlib import ExitStack

F32 = mybir.dt.float32
F16 = mybir.dt.float16
BF16 = mybir.dt.bfloat16
ALU = mybir.AluOpType
ACT = mybir.ActivationFunctionType
AX = mybir.AxisListType

P = 128
B, N, C, H = 8, 2048, 64, 128
T = N // P
TP = T // 2
W = 512
HALF = T // 2
Q = N // W
TQ = W // P
R = 16
NC_ = T * C
LAYERS = 3
LN_EPS = 1e-5
DEG_EPS = 1e-12
BN_EPS = 1e-5
NORM_FLOOR = 1e-12


def build(nc, x_in, adj, mask_in, ut, wscale, w0, w1, w2, wout, l2w, l3w, b0, b1, b2, bout, l2b, l3b,
          gamma, beta, ident_in, fold_in, pick_in, out):
    ctx = ExitStack()
    with ctx:
        def sb(name, shape, dt=F32):
            return ctx.enter_context(nc.sbuf_tensor(name, shape, dt))

        def sem(name):
            return ctx.enter_context(nc.semaphore(name))

        def sems(name, n):
            return [sem(f"{name}{i}") for i in range(n)]

        y_all = nc.dram_tensor("y_all", (B, P, NC_), F32).ap()
        x3_all = nc.dram_tensor("x3_all", (B, P, NC_), F32).ap()

        at = sb("at", [P, 2, T, N], F16)
        pair = sb("pair", [P, 2, 2, N], F16)
        col_ring = sb("col_ring", [P, Q, TQ, P])
        row_ring = sb("row_ring", [P, Q, W])
        y = sb("y", [P, NC_])
        gate = sb("gate", [P, 2, W])
        rows = sb("rows", [P, 2, W])
        ht = sb("ht", [P, N])
        x = sb("x", [P, NC_])
        y_sum = sb("y_sum", [P, B * C])
        y_sqs = sb("y_sqs", [P, B * C])
        count = sb("count", [P, B])
        over = sb("over", [P, B])
        xs = sb("xs", [P, T, P], F16)
        v = sb("v", [P, 2, C])
        ul = sb("ul", [P, N], BF16)
        ur = sb("ur", [P, N], BF16)
        ident = sb("ident", [P, P])
        ident16 = sb("ident16", [P, P], F16)
        fold = sb("fold", [C, C])
        pick = sb("pick", [P, 4])
        w0s = sb("w0s", [P, H])
        w1s = sb("w1s", [H, H])
        w2s = sb("w2s", [H, H])
        wouts = sb("wouts", [H, C])
        l2ws = sb("l2ws", [P, C])
        l3ws = sb("l3ws", [P, C])
        bias = sb("bias", [P, 2, H])
        cbias = sb("cbias", [P, 5, C])
        mask = sb("mask", [P, B * T])
        wsc = sb("wsc", [P, 1])
        warm = sb("warm", [P, 1])
        ones = sb("ones", [P, 1])
        part = sb("part", [P, 2, Q])
        deg = sb("deg", [P, 2, 2])
        half_neg = sb("half_neg", [P, HALF])
        d = sb("d", [P, T])
        wd = sb("wd", [P, T])
        mean = sb("mean", [P, T])
        rstd = sb("rstd", [P, 2, T])
        rounded = (y[:, :].bitcast(BF16), gate[:, :, :].rearrange("p a w -> p (a w)").bitcast(BF16))
        y_mean = v[:, 0, :]
        w0row = rows[:, 0, 0:H]
        tmp = rows[:, :, :].rearrange("p a w -> p (a w)")
        sq = gate[:, :, :].rearrange("p a w -> p (a w)")
        k_slot = pair[:, :, :, :].rearrange("p s h n -> p s (h n)").bitcast(F32)

        acc = ctx.enter_context(nc.psum_tensor("acc", [P, Q, W], F32))
        side = ctx.enter_context(nc.psum_tensor("side", [P, 2, 2, W], F32))
        turn, uu = side[:, :, 0, :], side[:, :, 1, :]

        u_in = sem("u_in")
        consts_in = sem("consts_in")
        const_made = sem("const_made")
        b0_in = sem("b0_in")
        u_step = sem("u_step")
        u_rounded = sem("u_rounded")
        col_in = sems("col_in", Q)
        row_in = sems("row_in", Q)
        x_in_done = sem("x_in_done")
        turned = sems("turned", Q)
        uu_done = sems("uu_done", Q)
        at_hi = sems("at_hi", Q)
        at_lo = sems("at_lo", Q)
        row_used = sems("row_used", Q)
        gated = sems("gated", Q)
        k_done = sems("k_done", Q)
        k_summed = sem("k_summed")
        k_used = sems("k_used", Q)
        row_hi = sems("row_hi", Q)
        row_lo = sems("row_lo", Q)
        deg_sum = sem("deg_sum")
        deg_done = sem("deg_done")
        d_done = sem("d_done")
        v_done = sem("v_done")
        slot_used = sems("slot_used", 2)
        at_used = sem("at_used")
        prod = sem("prod")
        evac = sem("evac")
        proj = sem("proj")
        hid_mm = sem("hid_mm")
        msg_mm = sem("msg_mm")
        msg_f = sem("msg_f")
        msg_hi = sem("msg_hi")
        msg_lo = sem("msg_lo")
        agg = sem("agg")
        relu = sem("relu")
        wd_done = sem("wd_done")
        e_scaled = sem("e_scaled")
        y_masked = sem("y_masked")
        y_summed = sem("y_summed")
        y_shift = sem("y_shift")
        y_diff = sem("y_diff")
        y_diff2 = sem("y_diff2")
        y_diff2m = sem("y_diff2m")
        y_stats = sem("y_stats")
        e_sum = sem("e_sum")
        res_step = sem("res_step")
        res_done = sem("res_done")
        cent_sum = sem("cent_sum")
        cent_mean = sem("cent_mean")
        cent_x = sem("cent_x")
        e_sq = sem("e_sq")
        e_var = sem("e_var")
        e_veps = sem("e_veps")
        e_inverse = sem("e_inverse")
        e_newton = sem("e_newton")
        e_rstd = sem("e_rstd")
        e_x = sem("e_x")
        x_hi = sem("x_hi")
        x_lo = sem("x_lo")
        y_bias = sem("y_bias")
        y_sq = sem("y_sq")
        y_var = sem("y_var")
        y_floor = sem("y_floor")
        y_rstd = sem("y_rstd")
        y_done = sem("y_done")
        y_out = sem("y_out")
        x3_out = sem("x3_out")
        fy_in = sems("fy_in", B)
        fx_in = sems("fx_in", B)
        f_dve = sem("f_dve")
        sums_ready = sem("sums_ready")
        sums_mm = sem("sums_mm")
        var_inverse = sem("var_inverse")
        var_root = sem("var_root")
        shift_ready = sem("shift_ready")
        z_scaled = sem("z_scaled")
        z_shifted = sem("z_shifted")
        z_masked = sem("z_masked")
        z_step = sem("z_step")
        z_mean = sem("z_mean")
        z_centred = sem("z_centred")
        z_sq = sem("z_sq")
        z_var = sem("z_var")
        z_inverse = sem("z_inverse")
        z_root = sem("z_root")
        z_newton = sem("z_newton")
        z_out = sem("z_out")
        f_out = sem("f_out")

        csum = part[:, 0, :]
        all_ones = w2s
        EPI = 3
        HC = HALF * C

        def half(ap, h):
            return ap[:, h * HC:(h + 1) * HC]

        def tiles(ap, h):
            return half(ap, h).rearrange("p (t c) -> p t c", c=C)

        def spread(ap, h):
            return ap[:, h * HALF:(h + 1) * HALF].unsqueeze(2).broadcast_to([P, HALF, C])

        def over_tiles(ap, n, w):
            return ap.unsqueeze(1).broadcast_to([P, n, w])

        def at_q(part_, i, q):
            return at[:, part_, bass.ds(i, 1), q * W:(q + 1) * W].rearrange("p a w -> p (a w)")

        def natural(e, h):
            bank = acc[:, h, :] if e == 3 else turn[:, h, :]
            return bank.rearrange("p (t c) -> p t c", c=C)

        def ring_block(s, q):
            return row_ring[:, q, :] if s == 0 else col_ring[:, q, :, :].rearrange("p t c -> p (t c)")

        PRODS = Q - 1 + Q

        N_CONSTS = 6 + 6 + 2 + 5 + 1 + 1
        W0_STEP = 8
        U_STEPS = W0_STEP + 3 * 4 + 3
        MEANS, INVERSE, ROOT, NEWTON = [9 * C + k * 2 * T for k in range(4)]

        OPEN = 1
        OPEN_K = 2

        def start_at_one(eng, *opened):
            for s in opened:
                eng.sem_inc(s, OPEN)

        block = ctx.enter_context(nc.Block())

        @block.sync
        def _(sp):
            def blocks(b, i, col_free, row_free):
                for q in range(Q):
                    for free, count in col_free:
                        sp.wait_ge(free[q], count)
                    sp.dma_start(col_ring[:, q, :, :],
                                 adj[bass.ds(b, 1), q * W:(q + 1) * W, bass.ds(i * P, P)]
                                 .rearrange("a (t p) c -> p (a t) c", p=P)).then_inc(col_in[q], 16)
                    for free, count in row_free:
                        sp.wait_ge(free[q], count)
                    sp.dma_start(row_ring[:, q, :], row_block(b, i, q)).then_inc(row_in[q], 16)

            def row_block(b, i, q):
                return adj[bass.ds(b, 1), bass.ds(i * P, P), q * W:(q + 1) * W].rearrange("a p c -> p (a c)")

            for dst, src in ((ident, ident_in), (fold, fold_in), (w1s, w1), (w2s, w2), (wouts, wout), (mask, mask_in)):
                sp.dma_start(dst[:, :], src).then_inc(consts_in, 16)
            for h in range(2):
                sp.dma_start(w0s[h * C:(h + 1) * C, :], w0).then_inc(consts_in, 16)
                sp.dma_start(l2ws[h * C:(h + 1) * C, :], l2w).then_inc(consts_in, 16)
                sp.dma_start(l3ws[h * C:(h + 1) * C, :], l3w).then_inc(consts_in, 16)
            for n, v in enumerate((b1, b2)):
                sp.dma_start(bias[:, n, :], v.partition_broadcast(P)).then_inc(consts_in, 16)
            for n, v in enumerate((bout, l2b, l3b, gamma, beta)):
                sp.dma_start(cbias[:, n, :], v.partition_broadcast(P)).then_inc(consts_in, 16)
            sp.dma_start(wsc[:, :], wscale.partition_broadcast(P)).then_inc(consts_in, 16)
            sp.dma_start(w0row, w0[C - 1, :].partition_broadcast(P)).then_inc(consts_in, 16)
            with sp.Fori(0, B) as b:
                last = [(row_lo, b * T + OPEN)]
                blocks(b, 0, last, last)
                blocks(b, 1, [(turned, b * T + 1 + OPEN)], [(row_used, b * T + 1 + OPEN)])
                sp.wait_ge(x3_out, (b + 1) * 16)
                sp.wait_ge(x_lo, b * 6 + OPEN)
                sp.dma_start(x[:, :], x_in[bass.ds(b, 1), :, :].rearrange("a p n -> p (a n)")).then_inc(x_in_done, 16)
                with sp.Fori(2, T) as i:
                    blocks(b, i, [(turned, b * T + i + OPEN)], [(row_used, b * T + i + OPEN)])
                for s in range(2):
                    for q in range(Q):
                        sp.wait_ge((row_used if s == 0 else turned)[q], (b + 1) * T + OPEN)
                        sp.dma_start(ring_block(s, q), row_block(b, s, q)).then_inc((row_in if s == 0 else col_in)[q], 16)
                with sp.Fori(1, TP) as jj:
                    for s in range(2):
                        for q in range(Q):
                            sp.wait_ge(row_lo[q], b * T + jj * 2 + s - 1 + OPEN)
                            sp.dma_start(ring_block(s, q), row_block(b, jj * 2 + s, q))\
                              .then_inc((row_in if s == 0 else col_in)[q], 16)
            yf = at[:, 0, 0:8, :].rearrange("p a n -> p (a n)").bitcast(F32)
            xf = at[:, 0, 8:16, :].rearrange("p a n -> p (a n)").bitcast(F32)
            sp.wait_ge(y_out, 16 * (B + 1))
            sp.wait_ge(x3_out, 16 * (B + 1))
            sp.wait_ge(at_used, B * T + T)
            for b in range(B):
                sp.dma_start(yf[:, b * NC_:(b + 1) * NC_], y_all[b]).then_inc(fy_in[b], 16)
            for b in range(B):
                sp.dma_start(xf[:, b * NC_:(b + 1) * NC_], x3_all[b]).then_inc(fx_in[b], 16)
            for b in range(B):
                sp.wait_ge(z_out, b + 1)
                sp.dma_start(out[b], xf[:, b * NC_:(b + 1) * NC_]).then_inc(f_out, 16)
            sp.wait_ge(f_out, 16 * B)


        @block.tensor
        def _(pe):
            def unit(b, i, q):
                n = b * T + i
                pe.wait_ge(col_in[q], (b * (T + TP) + i + 1) * 16)
                before, more = (q + 2) % Q, int(q >= 2)
                pe.wait_ge(at_lo[before], n + more + OPEN)
                for t in range(TQ):
                    mm = nc.tensor.transpose(turn[:, q % 2, t * P:(t + 1) * P], col_ring[:, q, t, :], ident[:, :])
                mm.then_inc(turned[q], 1)
                pe.wait_ge(gated[before], n + more + OPEN)
                nc.tensor.matmul(uu[:, q % 2, :], ul[:, bass.ds(i * P, P)], ur[:, q * W:(q + 1) * W],
                                 start=True, stop=True).then_inc(uu_done[q], 1)

            def k_product(n, s, q, first=False, last=False):
                pe.wait_ge(v_done, n + 1)
                mm = nc.tensor.matmul(acc[0:C, q, :], v[:, s, :], k_slot[:, s, q * W:(q + 1) * W],
                                      start=first, stop=last)
                mm.then_inc(k_used[q], 1)

            def project(e, weights, c):
                k = C if e == 0 else P
                for t in range(c * TQ, (c + 1) * TQ):
                    mm = nc.tensor.matmul(natural(e, t // HALF)[:, t % HALF, :], ht[0:k, t * P:(t + 1) * P],
                                          weights, start=True, stop=True)
                if c % 2:
                    mm.then_inc(proj, 1)

            def project_all(e, b, weights):
                for c in range(Q):
                    pe.wait_ge(evac, (b * 4 + e) * Q + (Q if e == 3 else c + 1))
                    project(e, weights, c)

            def hidden(b, c):
                pe.wait_ge(evac, (b * 4 + 1) * Q + c + 1)
                nc.tensor.matmul(uu[:, c % 2, :], w0s[:, :], ht[:, c * W:(c + 1) * W], start=True, stop=True)\
                  .then_inc(hid_mm, 1)

            def messages(b, k, c):
                pe.wait_ge(relu, (b * LAYERS + k - 1) * Q + c + 1)
                n = (b * 2 + k - 1) * Q + c
                if k > 1 or c >= 2:
                    pe.wait_ge(msg_f, n - 1)
                for t in range(TQ):
                    a = (c * TQ + t) * P
                    mm = nc.tensor.matmul(turn[:, c % 2, t * H:(t + 1) * H], ht[:, a:a + P], (w1s, w2s)[k - 1][:, :],
                                          start=True, stop=True)
                mm.then_inc(msg_mm, 1)

            def agg_step(b, k, c, j, start=False, stop=False):
                s = k - 1
                hi = pair[:, s, 0, bass.ds(j * P, P)]
                lo = pair[:, s, 1, bass.ds(j * P, P)]
                nc.tensor.matmul(acc[:, c, :], hi, at_q(0, j, c), start=start, stop=False)
                nc.tensor.matmul(acc[:, c, :], hi, at_q(1, j, c), start=False, stop=False)
                return nc.tensor.matmul(acc[:, c, :], lo, at_q(0, j, c), start=False, stop=stop)

            def aggregate(b, k, c):
                agg_step(b, k, c, 0, start=True)
                with pe.Fori(1, T - 1, 2) as j:
                    agg_step(b, k, c, j)
                    agg_step(b, k, c, j + 1)
                agg_step(b, k, c, T - 1, stop=True).then_inc(agg, 1)

            def aggregate_tiles(b, k, c, g):
                for j in range(g * TQ, (g + 1) * TQ):
                    mm = agg_step(b, k, c, j, start=(j == 0), stop=(j == T - 1))
                if g == Q - 1:
                    mm.then_inc(agg, 1)

            def first_aggregates(b, k, between):
                for g in range(2):
                    pe.wait_ge(msg_lo, (b * 2 + k - 1) * Q + g + 1)
                    aggregate_tiles(b, k, 0, g)
                    for step in between[g]:
                        step()
                for g in range(2):
                    aggregate_tiles(b, k, 1, g)
                for g in range(2, Q):
                    pe.wait_ge(msg_lo, (b * 2 + k - 1) * Q + g + 1)
                    for c in range(2):
                        aggregate_tiles(b, k, c, g)

            def x_step(i, c, h, start=False, stop=False):
                xi = xs[:, bass.ds(i, 1), :].rearrange("p a c -> p (a c)")
                return nc.tensor.matmul(acc[:, c, :], xi, at_q(h, i, c), start=start, stop=stop)

            def x_steps(c, lo, hi):
                for k in range(2):
                    x_step(lo, c + k, 0, start=(lo == 0))
                    x_step(lo, c + k, 1)
                with pe.Fori(lo + 1, min(hi, T - 1)) as i:
                    for k in range(2):
                        x_step(i, c + k, 0)
                        x_step(i, c + k, 1)
                if hi == T:
                    for k in range(2):
                        x_step(T - 1, c + k, 0)
                        x_step(T - 1, c + k, 1, stop=True).then_inc(agg, 1)

            def row_product(b, i, s, first=False, last=False):
                for q in range(Q):
                    pe.wait_ge(row_lo[q], b * T + i + 1 + OPEN)
                    for h in range(2):
                        mm = nc.tensor.matmul(acc[:, q, :], xs[:, bass.ds(i, 1), :].rearrange("p a c -> p (a c)"),
                                              pair[:, s, h, q * W:(q + 1) * W],
                                              start=(first and h == 0), stop=(last and h == 1))
                    if last and q < Q - 1:
                        mm.then_inc(prod, 1)
                mm.then_inc(slot_used[s], 1)

            def at_product(i, first=False):
                for q in range(Q):
                    x_step(i, q, 0, start=first)
                    mm = x_step(i, q, 1)
                mm.then_inc(at_used, 1)

            def at_products(lo, hi):
                with pe.Fori(lo, hi) as i:
                    at_product(i)

            def layer_3(b, more):
                pe.wait_ge(x_lo, b * 6 + 5 + OPEN)
                at_product(0, first=True)
                for k in range(2 * Q):
                    if more:
                        if k == 1:
                            pe.wait_ge(e_sum, (b + 1) * 2 * EPI)
                        unit(b + 1, k // Q, k % Q)
                    if k == 2 * Q - 1:
                        pe.wait_ge(x_lo, b * 6 + 6 + OPEN)
                    at_product(1 + k)
                at_products(2 * Q + 1, T)
                for t in range(T):
                    mm = nc.tensor.matmul(acc[:, t // TQ, t % TQ * P:(t % TQ + 1) * P], xs[:, t, :], ident16[:, :],
                                          start=False, stop=(t % TQ == TQ - 1))
                    if t % TQ == TQ - 1:
                        mm.then_inc(prod, 1)
                if more:
                    for q in range(2):
                        unit(b + 1, 2, q)
                project_all(3, b, l3ws[:, :])
                if more:
                    two_stripes(b + 1, 1, first=True)

            def two_stripes(b, jj, first=False, wait_y=True):
                n = b * T + jj * 2
                if first:
                    if wait_y:
                        pe.wait_ge(y_bias, b * 2 + OPEN)
                    k_product(n - 2, 0, 0, first=True)
                for s in range(2):
                    for q in range(Q):
                        if not (first and s == 0 and q < 2):
                            unit(b, jj * 2 + s, q)
                        if q < Q - 1:
                            k_product(n + s - 2, s, q + 1, first=(first and s == 0))
                        else:
                            k_product(n + s - 1, 1 - s, 0)

            def layers_0_to_2(b):
                n = b * T
                with pe.Fori(2, TP) as jj:
                    two_stripes(b, jj)
                for q in range(1, Q):
                    k_product(n + T - 2, 0, q)
                for q in range(Q):
                    k_product(n + T - 1, 1, q, last=True)
                pe.wait_ge(at_lo[3], (b + 1) * T + OPEN)
                project_all(0, b, fold[:, :])
                if type(b) is int and b == 0:
                    pe.wait_ge(u_step, U_STEPS)
                pe.wait_ge(x_lo, b * 6 + 1 + OPEN)
                pe.wait_ge(gated[3], (b + 1) * T + OPEN)
                x_steps(0, 0, HALF)
                pe.wait_ge(x_lo, b * 6 + 2 + OPEN)
                x_steps(0, HALF, T)
                x_steps(2, 0, HALF)
                hidden(b, 0)
                hidden(b, 1)
                x_steps(2, HALF, HALF + 3)
                messages(b, 1, 0)
                messages(b, 1, 1)
                x_steps(2, HALF + 3, T)
                first_aggregates(b, 1, [[lambda: hidden(b, 2), lambda: hidden(b, 3)],
                                        [lambda: messages(b, 1, 2), lambda: messages(b, 1, 3)]])
                aggregate(b, 1, 2)
                messages(b, 2, 0)
                messages(b, 2, 1)
                aggregate(b, 1, 3)
                messages(b, 2, 2)
                first_aggregates(b, 2, [[lambda: messages(b, 2, 3)], []])
                aggregate(b, 2, 2)
                pe.wait_ge(msg_f, (b + 1) * 2 * Q)
                for c in range(Q):
                    if c == 2:
                        aggregate(b, 2, 3)
                    pe.wait_ge(relu, (b * LAYERS + 2) * Q + c + 1)
                    project(1, wouts[:, :], c)
                pe.wait_ge(x_lo, b * 6 + 3 + OPEN)
                row_product(b, 0, 0, first=True)
                row_product(b, 1, 1)
                with pe.Fori(1, TP // 2) as jj:
                    row_product(b, jj * 2, 0)
                    row_product(b, jj * 2 + 1, 1)
                pe.wait_ge(x_lo, b * 6 + 4 + OPEN)
                row_product(b, HALF, 0)
                row_product(b, HALF + 1, 1)
                with pe.Fori(TP // 2 + 1, TP - 1) as jj:
                    row_product(b, jj * 2, 0)
                    row_product(b, jj * 2 + 1, 1)
                row_product(b, T - 2, 0)
                row_product(b, T - 1, 1, last=True)
                project_all(2, b, l2ws[:, :])

            start_at_one(pe, *turned, *slot_used)
            for used in k_used:
                pe.sem_inc(used, OPEN_K)
            pe.sem_inc(at_used, T)
            pe.wait_ge(u_step, W0_STEP - 1)
            pe.wait_ge(const_made, 1)
            for k in range(2 * Q + 2):
                unit(0, k // Q, k % Q)
            two_stripes(0, 1, first=True, wait_y=False)
            pe.wait_ge(b0_in, 32)
            layers_0_to_2(0)
            with pe.Fori(1, B) as b:
                layer_3(b - 1, True)
                layers_0_to_2(b)
            layer_3(B - 1, False)

            pe.wait_ge(const_made, 2)
            pe.wait_ge(sums_ready, 1)
            nc.tensor.matmul(acc[:, 0, 0:C + 1], all_ones[:, :], ht[:, 0:C + 1], start=True, stop=True).then_inc(sums_mm, 1)
            pe.wait_ge(sums_ready, 2)
            nc.tensor.matmul(acc[:, 1, 0:C], all_ones[:, :], ht[:, 2 * C:3 * C], start=True, stop=True).then_inc(sums_mm, 1)

        @block.scalar
        def _(act):
            def head(b, i, q):
                n = b * T + i
                act.wait_ge(turned[q], n + 1 + OPEN)
                if q == 0:
                    act.wait_ge(at_used, n + 1)
                nc.scalar.activation(at_q(0, i, q), turn[:, q % 2, :], ACT.Copy).then_inc(at_hi[q], 1)
                act.wait_ge(uu_done[q], n + 1)
                act.wait_ge(k_done[(q + 2) % Q], n + int(q >= 2) + OPEN)
                nc.scalar.activation(gate[:, q % 2, :], uu[:, q % 2, :], ACT.Sigmoid).then_inc(gated[q], 1)

            def k_sum(n, s, q):
                act.wait_ge(k_done[q], n + 1 + OPEN)
                k = k_slot[:, s, q * W:(q + 1) * W]
                nc.scalar.activation(k, k, ACT.Copy, accum_out=part[:, s, q:q + 1]).then_inc(k_summed, 1)

            def pair_of_stripes(b, jj, last):
                for s in range(2):
                    i = jj * 2 + s
                    head(b, i, 1)
                    head(b, i, 2)
                    k_sum(b * T + i, s, 0)
                    head(b, i, 3)
                    if not (last and s == 1):
                        head(b, i + 1, 0)
                    k_sum(b * T + i, s, 2)

            def squares(b, e, h):
                act.wait_ge(e_sum, b * 2 * EPI + 2 * e + h + 1)
                nc.scalar.activation(half(sq, h), half(tmp, h), ACT.Square).then_inc(e_sq, 1)

            def root(b, e, h):
                r = slice(h * HALF, (h + 1) * HALF)
                act.wait_ge(e_inverse, b * 2 * EPI + 2 * e + h + 1)
                nc.scalar.activation(rstd[:, 1, r], rstd[:, 0, r], ACT.Sqrt).then_inc(e_rstd, 1)

            def x_high(b, e, h):
                keep = C - 1 if e == 0 else C
                act.wait_ge(e_x, b * 2 * EPI + 2 * e + h + 1)
                nc.scalar.activation(xs[:, h * HALF:(h + 1) * HALF, 0:keep], tiles(x, h)[:, :, 0:keep], ACT.Copy)\
                  .then_inc(x_hi, 1)

            def norm_steps(b, e, h):
                squares(b, e, h)
                root(b, e, h)
                x_high(b, e, h)

            def evacuate(b, e, c):
                if e == 0:
                    act.wait_ge(k_used[c], (b + 1) * T + OPEN_K)
                elif e == 1:
                    act.wait_ge(agg, b * LAYERS * Q + c + 1)
                elif e == 2:
                    if c < Q - 1:
                        act.wait_ge(prod, b * PRODS + c + 1)
                    else:
                        act.wait_ge(slot_used[1], (b + 1) * TP + OPEN)
                else:
                    act.wait_ge(prod, b * PRODS + Q - 1 + c + 1)
                rows_ = slice(0, C if e == 0 else P)
                nc.scalar.activation(ht[rows_, c * W:(c + 1) * W], acc[rows_, c, :], ACT.Copy).then_inc(evac, 1)

            def rectify(b, k, c):
                if k == 0:
                    act.wait_ge(hid_mm, b * Q + c + 1)
                else:
                    act.wait_ge(agg, (b * LAYERS + k) * Q + c + 1)
                nc.scalar.activation(ht[:, c * W:(c + 1) * W], uu[:, c % 2, :] if k == 0 else acc[:, c, :],
                                     ACT.Relu).then_inc(relu, 1)

            def message_high(b, k, c):
                act.wait_ge(msg_f, (b * 2 + k - 1) * Q + c + 1)
                nc.scalar.activation(pair[:, k - 1, 0, c * W:(c + 1) * W], rows[:, c % 2, :], ACT.Copy).then_inc(msg_hi, 1)

            def row_high(b, jj, s, q):
                act.wait_ge((row_in if s == 0 else col_in)[q], (b * (T + TP) + T + jj + 1) * 16)
                if q == 0:
                    act.wait_ge(agg, (b * LAYERS + 2 + s) * Q)
                    act.wait_ge(slot_used[s], b * TP + jj + OPEN)
                nc.scalar.activation(pair[:, s, 0, q * W:(q + 1) * W], ring_block(s, q), ACT.Copy).then_inc(row_hi[q], 1)

            def stats(b):
                act.wait_ge(y_diff, b + 1)
                nc.scalar.activation(sq, sq, ACT.Square).then_inc(y_diff2, 1)

            def layers_0_to_2(b, with_stats=False):
                with act.Fori(2, TP - 1) as jj:
                    pair_of_stripes(b, jj, False)
                pair_of_stripes(b, TP - 1, True)
                nc.scalar.activation(warm[:, :], ones[:, 0:1], ACT.Sqrt)
                for c in range(Q):
                    evacuate(b, 0, c)
                for h in range(2):
                    norm_steps(b, 0, h)
                for c in range(0, Q, 2):
                    evacuate(b, 1, c)
                    evacuate(b, 1, c + 1)
                    rectify(b, 0, c)
                    rectify(b, 0, c + 1)
                    message_high(b, 1, c)
                    message_high(b, 1, c + 1)
                rectify(b, 1, 0)
                rectify(b, 1, 1)
                if with_stats:
                    stats(b - 1)
                rectify(b, 1, 2)
                message_high(b, 2, 0)
                message_high(b, 2, 1)
                rectify(b, 1, 3)
                message_high(b, 2, 2)
                message_high(b, 2, 3)
                for q in range(Q):
                    row_high(b, 0, 0, q)
                rectify(b, 2, 0)
                rectify(b, 2, 1)
                norm_steps(b, 1, 0)
                rectify(b, 2, 2)
                rectify(b, 2, 3)
                for q in range(Q):
                    row_high(b, 0, 1, q)
                squares(b, 1, 1)
                row_high(b, 1, 0, 0)
                row_high(b, 1, 0, 1)
                root(b, 1, 1)
                row_high(b, 1, 0, 2)
                row_high(b, 1, 0, 3)
                row_high(b, 1, 1, 0)
                x_high(b, 1, 1)
                for q in range(1, Q):
                    row_high(b, 1, 1, q)
                with act.Fori(2, TP) as jj:
                    for s in range(2):
                        for q in range(Q):
                            row_high(b, jj, s, q)
                for c in range(Q):
                    evacuate(b, 2, c)
                for h in range(2):
                    norm_steps(b, 2, h)
                act.dma_start(x3_all[bass.ds(b, 1), :, :].rearrange("a p n -> p (a n)"), x[:, :]).then_inc(x3_out, 16)

            def layer_3(b, more):
                if more:
                    nc.scalar.activation(warm[:, :], ones[:, 0:1], ACT.Sigmoid)
                    head(b + 1, 0, 0)
                    pair_of_stripes(b + 1, 0, True)
                for c in range(Q):
                    evacuate(b, 3, c)
                if more:
                    head(b + 1, 2, 0)
                for h in range(2):
                    act.wait_ge(y_bias, b * 2 + h + 1 + OPEN)
                    nc.scalar.activation(half(tmp, h), half(y, h), ACT.Square).then_inc(y_sq, 1)
                if more:
                    pair_of_stripes(b + 1, 1, False)
                act.wait_ge(y_done, b * 2 + 2)
                act.dma_start(y_all[bass.ds(b, 1), :, :].rearrange("a p n -> p (a n)"), y[:, :]).then_inc(y_out, 16)

            start_at_one(act, *gated)
            act.sem_inc(x3_out, 16)
            act.sem_inc(y_out, 16)
            act.dma_start(pick[:, :], pick_in).then_inc(u_in, 16)
            for g in range(P // R):
                act.dma_start(ht[g * R:(g + 1) * R, :], ut).then_inc(u_in, 16)
            for lr in range(2):
                act.wait_ge(u_step, 4 + lr)
                nc.scalar.activation(rounded[lr], k_slot[:, lr, :], ACT.Copy).then_inc(u_rounded, 1)
            act.wait_ge(consts_in, N_CONSTS * 16)
            nc.scalar.activation(ident16[:, :], ident[:, :], ACT.Copy).then_inc(const_made, 1)
            head(0, 0, 0)
            pair_of_stripes(0, 0, True)
            act.wait_ge(u_step, W0_STEP)
            for h in range(2):
                act.dma_start(w0s[(h + 1) * C - 1:(h + 1) * C, :], b0.rearrange("(a h) -> a h", a=1)).then_inc(b0_in, 16)
            head(0, 2, 0)
            pair_of_stripes(0, 1, False)
            layers_0_to_2(0)
            with act.Fori(1, B) as b:
                layer_3(b - 1, True)
                layers_0_to_2(b, True)
            layer_3(B - 1, False)
            stats(B - 1)
            xf = at[:, 0, 8:16, :].rearrange("p a n -> p (a n)").bitcast(F32)
            sqf = at[:, 1, 0:8, :].rearrange("p a n -> p (a n)").bitcast(F32)
            act.wait_ge(var_inverse, 1)
            nc.scalar.activation(ht[:, 4 * C:5 * C], ht[:, 3 * C:4 * C], ACT.Sqrt).then_inc(var_root, 1)

            def z_squares(b):
                act.wait_ge(z_centred, b + 1)
                nc.scalar.activation(sqf[:, b * NC_:(b + 1) * NC_], xf[:, b * NC_:(b + 1) * NC_], ACT.Square)\
                  .then_inc(z_sq, 1)

            z_squares(0)
            for b in range(B):
                if b + 1 < B:
                    z_squares(b + 1)
                act.wait_ge(z_inverse, b + 1)
                w = b % 2 * T
                nc.scalar.activation(ht[:, ROOT + w:ROOT + w + T], ht[:, INVERSE + w:INVERSE + w + T], ACT.Sqrt)\
                  .then_inc(z_root, 1)

        @block.vector
        def _(dve):
            def unit(b, jj, s, q, first=False):
                i = jj * 2 + s
                n = b * T + i
                dve.wait_ge(row_in[q], (b * (T + TP) + i + 1) * 16)
                dve.wait_ge(at_hi[q], n + 1)
                if first and q == 0:
                    dve.wait_ge(slot_used[s], b * TP + OPEN)
                dve.wait_ge(k_used[q], n - 1 + OPEN_K)
                k = k_slot[:, s, q * W:(q + 1) * W]
                nc.vector.tensor_tensor(k, row_ring[:, q, :], turn[:, q % 2, :], ALU.add).then_inc(row_used[q], 1)
                nc.vector.tensor_tensor(at_q(1, i, q), turn[:, q % 2, :], at_q(0, i, q), ALU.subtract)\
                  .then_inc(at_lo[q], 1)
                if q % 2:
                    dve.wait_ge(row_used[q], n + 1 + OPEN)
                    dve.wait_ge(gated[q], n + 1 + OPEN)
                    nc.vector.scalar_tensor_tensor(k, k, 1.0, gate[:, 1, :], ALU.mult, ALU.mult,
                                                   accum_out=part[:, s, q:q + 1]).then_inc(k_done[q], 1)

            def degree(n, s):
                for q in (1, 3):
                    dve.wait_ge(k_done[q], n + 1 + OPEN)
                dve.wait_ge(k_summed, (n + 1) * 2)
                nc.vector.tensor_reduce(deg[:, s, 0:1], part[:, s, :], AX.X, ALU.add).then_inc(deg_sum, 1)
                dve.wait_ge(deg_sum, n + 1)
                nc.vector.tensor_scalar(deg[:, s, 1:2], deg[:, s, 0:1], 0.5, DEG_EPS, ALU.mult, ALU.max)\
                  .then_inc(deg_done, 1)

            u = [0]

            def u_next(ins):
                u[0] += 1
                ins.then_inc(u_step, 1)
                dve.wait_ge(u_step, u[0])

            def mean_x(b):
                dve.wait_ge(x_in_done, (b + 1) * 16)
                nc.vector.tensor_reduce(mean[:, :], x[:, :].rearrange("p (t c) -> p t c", c=C), AX.X, ALU.add)\
                  .then_inc(cent_sum, 1)
                dve.wait_ge(cent_sum, b + 1)
                nc.vector.tensor_scalar(mean[:, :], mean[:, :], -1.0 / C, None, ALU.mult).then_inc(cent_mean, 1)
                dve.wait_ge(cent_mean, b + 1)

            def norm(b, e, rows_between=False):
                nth = b * 2 * EPI + 2 * e + 1

                def scaled(h):
                    dve.wait_ge(proj, b * 8 + 2 * e + h + 1)
                    if e == 0:
                        nc.vector.tensor_tensor(tiles(tmp, h), natural(e, h), spread(wd, h), ALU.mult).then_inc(e_scaled, 1)
                    elif e == 1:
                        m = mask[:, bass.ds(b * T + h * HALF, HALF)].unsqueeze(2).broadcast_to([P, HALF, C])
                        nc.vector.tensor_tensor(tiles(tmp, h), natural(e, h), m, ALU.mult).then_inc(e_scaled, 1)

                def summed(h):
                    if e < 2:
                        dve.wait_ge(e_scaled, b * 4 + 2 * e + h + 1)
                    if e == 0:
                        dve.wait_ge(cent_x, b + 1)
                    elif h == 0:
                        dve.wait_ge(res_done, b * 2 + e)
                    nc.vector.tensor_tensor(half(tmp, h), half(tmp, h) if e < 2 else turn[:, h, :], half(x, h),
                                            ALU.add).then_inc(e_sum, 1)

                def variance(h):
                    r = rstd[:, 0, h * HALF:(h + 1) * HALF]
                    dve.wait_ge(e_sq, nth + h)
                    nc.vector.tensor_reduce(r, tiles(sq, h), AX.X, ALU.add).then_inc(e_var, 1)
                    dve.wait_ge(e_var, nth + h)
                    nc.vector.tensor_scalar(r, r, 1.0 / C, LN_EPS, ALU.mult, ALU.add).then_inc(e_veps, 1)
                    dve.wait_ge(e_veps, nth + h)
                    nc.vector.reciprocal(r, r).then_inc(e_inverse, 1)

                def deviation(h):
                    root = rstd[:, 1, h * HALF:(h + 1) * HALF]
                    other = mean[:, h * HALF:(h + 1) * HALF]
                    dve.wait_ge(e_rstd, nth + h)
                    step = 3 * (nth + h - 1)
                    nc.vector.reciprocal(other, root).then_inc(e_newton, 1)
                    dve.wait_ge(e_newton, step + 1)
                    nc.vector.tensor_tensor(other, other, rstd[:, 0, h * HALF:(h + 1) * HALF], ALU.mult).then_inc(e_newton, 1)
                    dve.wait_ge(e_newton, step + 2)
                    nc.vector.tensor_tensor(root, root, other, ALU.add).then_inc(e_newton, 1)

                def normed(h):
                    dve.wait_ge(e_newton, 3 * (nth + h))
                    nc.vector.scalar_tensor_tensor(tiles(x, h), tiles(tmp, h), 0.5, spread(rstd[:, 1, :], h), ALU.mult,
                                                   ALU.mult).then_inc(e_x, 1)

                def low(h):
                    keep = C - 1 if e == 0 else C
                    s = slice(h * HALF, (h + 1) * HALF)
                    if e == 0:
                        nc.vector.memset(xs[:, s, C - 1:C], 1.0)
                        nc.vector.memset(xs[:, s, P - 1:P], 0.0)
                    dve.wait_ge(x_hi, b * 6 + 2 * e + h + 1)
                    nc.vector.tensor_tensor(xs[:, s, C:C + keep], tiles(x, h)[:, :, 0:keep], xs[:, s, 0:keep],
                                            ALU.subtract).then_inc(x_lo, 1)

                scaled(0)
                summed(0)
                variance(0)
                deviation(0)
                normed(0)
                if e == 0:
                    scaled(1)
                low(0)
                if rows_between:
                    for q in range(Q):
                        row_low(b, 1, 1, q)
                if e > 0:
                    scaled(1)
                summed(1)
                if rows_between:
                    row_low(b, 2, 0, 0)
                    row_low(b, 2, 0, 1)
                variance(1)
                if rows_between:
                    row_low(b, 2, 0, 2)
                    row_low(b, 2, 0, 3)
                deviation(1)
                normed(1)
                if rows_between:
                    row_low(b, 3, 1, 0)
                low(1)
                if rows_between:
                    for q in range(1, Q):
                        row_low(b, 3, 1, q)

            def message(b, k, c):
                n = (b * 2 + k - 1) * Q + c
                dve.wait_ge(msg_mm, n + 1)
                nc.vector.tensor_tensor(rows[:, c % 2, :].rearrange("p (t h) -> p t h", h=H),
                                        turn[:, c % 2, :].rearrange("p (t h) -> p t h", h=H),
                                        over_tiles(bias[:, k - 1, :], TQ, H), ALU.add).then_inc(msg_f, 1)
                dve.wait_ge(msg_f, n + 1)
                dve.wait_ge(msg_hi, n + 1)
                cols = slice(c * W, (c + 1) * W)
                nc.vector.tensor_tensor(pair[:, k - 1, 1, cols], rows[:, c % 2, :], pair[:, k - 1, 0, cols],
                                        ALU.subtract).then_inc(msg_lo, 1)

            def row_low(b, i, s, q):
                dve.wait_ge(row_hi[q], b * T + i + 1)
                cols = slice(q * W, (q + 1) * W)
                nc.vector.tensor_tensor(pair[:, s, 1, cols], ring_block(s, q), pair[:, s, 0, cols], ALU.subtract)\
                  .then_inc(row_lo[q], 1)

            def stripe(b, jj, s, first=False, start=False):
                unit(b, jj, s, 0, first=first)
                if not start:
                    degree(b * T + jj * 2 + s - 1, 1 - s)
                for q in range(1, Q):
                    unit(b, jj, s, q)

            def y_sums(b):
                dve.wait_ge(y_masked, b + 1)
                sums = y_sum[:, bass.ds(b * C, C)]
                nc.vector.tensor_reduce(sums, sq.rearrange("p (t c) -> p c t", c=C), AX.X, ALU.add).then_inc(y_summed, 1)
                dve.wait_ge(y_summed, b + 1)
                nc.vector.scalar_tensor_tensor(y_mean, sums, -1.0, over[:, bass.ds(b, 1)].broadcast_to([P, C]),
                                               ALU.mult, ALU.mult).then_inc(y_shift, 1)

            def y_squares(b):
                sq_tiles = sq.rearrange("p (t c) -> p t c", c=C)
                dve.wait_ge(y_diff2, b + 1)
                nc.vector.tensor_tensor(sq_tiles, sq_tiles, mask[:, bass.ds(b * T, T)].unsqueeze(2).broadcast_to([P, T, C]),
                                        ALU.mult).then_inc(y_diff2m, 1)
                dve.wait_ge(y_diff2m, b + 1)
                nc.vector.tensor_reduce(y_sqs[:, bass.ds(b * C, C)], sq.rearrange("p (t c) -> p c t", c=C), AX.X, ALU.add)\
                  .then_inc(y_stats, 1)

            def finish_weights():
                for w in (wouts[:, :], l2ws[:, :], cbias[:, 0, :], cbias[:, 1, :]):
                    u_next(nc.vector.tensor_reduce(csum[:, 0:1], w, AX.X, ALU.add))
                    u_next(nc.vector.tensor_scalar(csum[:, 1:2], csum[:, 0:1], -1.0 / C, None, ALU.mult))
                    u_next(nc.vector.tensor_scalar(w, w, csum[:, 1:2], None, ALU.add))
                u_next(nc.vector.tensor_reduce(count[:, :], mask[:, :].rearrange("p (b t) -> p b t", t=T), AX.X, ALU.add))
                u_next(nc.vector.tensor_scalar(over[:, :], count[:, :], 1.0, None, ALU.max))
                u_next(nc.vector.reciprocal(over[:, :], over[:, :]))
                assert u[0] == U_STEPS

            def layers_0_to_2(b, with_stats=False):
                with dve.Fori(2, TP) as jj:
                    for s in range(2):
                        stripe(b, jj, s)
                degree((b + 1) * T - 1, 1)
                if type(b) is int and b == 0:
                    finish_weights()
                dve.wait_ge(v_done, (b + 1) * T)
                nc.vector.tensor_scalar(wd[:, :], d[:, :], wsc[:, :], 0.5, ALU.mult, ALU.mult).then_inc(wd_done, 1)
                dve.wait_ge(wd_done, b + 1)
                for h in range(2):
                    ins = nc.vector.tensor_tensor(tiles(x, h), tiles(x, h), spread(mean, h), ALU.add)
                ins.then_inc(cent_x, 1)
                norm(b, 0)
                for c in range(Q):
                    message(b, 1, c)
                if with_stats:
                    y_sums(b - 1)
                for c in range(Q):
                    message(b, 2, c)
                if with_stats:
                    y_squares(b - 1)
                for q in range(Q):
                    row_low(b, 0, 0, q)
                norm(b, 1, rows_between=True)
                with dve.Fori(2, TP) as jj:
                    for s in range(2):
                        for q in range(Q):
                            row_low(b, jj * 2 + s, s, q)
                norm(b, 2)

            def layer_3(b, more):
                if more:
                    for s in range(2):
                        stripe(b + 1, 0, s, first=True, start=(s == 0))
                    mean_x(b + 1)
                for h in range(2):
                    dve.wait_ge(proj, b * 8 + 6 + h + 1)
                    if h == 0:
                        dve.wait_ge(y_out, (b + 1) * 16)
                    nc.vector.tensor_tensor(tiles(y, h), natural(3, h), over_tiles(cbias[:, 2, :], HALF, C),
                                            ALU.add).then_inc(y_bias, 1)
                if more:
                    stripe(b + 1, 1, 0)
                for h in range(2):
                    r = rstd[:, 0, h * HALF:(h + 1) * HALF]
                    dve.wait_ge(y_sq, b * 2 + h + 1)
                    nc.vector.tensor_reduce(r, tiles(tmp, h), AX.X, ALU.add).then_inc(y_var, 1)
                    dve.wait_ge(y_var, b * 2 + h + 1)
                    nc.vector.tensor_scalar(r, r, NORM_FLOOR ** 2, None, ALU.max).then_inc(y_floor, 1)
                if more:
                    stripe(b + 1, 1, 1)
                for h in range(2):
                    dve.wait_ge(y_rstd, b * 2 + h + 1)
                    nc.vector.tensor_tensor(tiles(y, h), tiles(y, h), spread(rstd[:, 1, :], h), ALU.mult)\
                      .then_inc(y_done, 1)

            start_at_one(dve, *row_used, *row_lo, *at_lo, k_done[1], k_done[3], x_lo, y_bias)
            u_next(nc.vector.memset(ones[:, :], 1.0))
            u_next(nc.vector.memset(half_neg[:, :], -0.5))
            dve.wait_ge(u_in, (1 + P // R) * 16)
            h1 = xs[:, :, :].rearrange("p t c -> p (t c)").bitcast(BF16)
            u_next(nc.vector.tensor_copy(h1, ht[:, :]))
            for lr in range(2):
                u_next(nc.vector.scalar_tensor_tensor(k_slot[:, lr, :], h1, pick[:, 2 * lr:2 * lr + 1], ht[:, :],
                                                      ALU.mult, ALU.add))
            for lr, dst in ((0, ul), (1, ur)):
                dve.wait_ge(u_rounded, lr + 1)
                u_next(nc.vector.scalar_tensor_tensor(dst[:, :], rounded[lr], pick[:, 2 * lr + 1:2 * lr + 2],
                                                      k_slot[:, lr, :], ALU.mult, ALU.add))
            dve.wait_ge(consts_in, N_CONSTS * 16)
            u_next(nc.vector.tensor_tensor(w0s[:, :], w0s[:, :], w0row, ALU.subtract))

            for jj in range(2):
                for s in range(2):
                    stripe(0, jj, s, first=(jj == 0), start=(jj + s == 0))
                if jj == 0:
                    mean_x(0)
            layers_0_to_2(0)
            with dve.Fori(1, B) as b:
                layer_3(b - 1, True)
                layers_0_to_2(b, True)
            layer_3(B - 1, False)

            nc.vector.memset(all_ones[:, :], 1.0).then_inc(const_made, 1)
            y_sums(B - 1)

            yf = at[:, 0, 0:8, :].rearrange("p a n -> p (a n)").bitcast(F32)
            xf = at[:, 0, 8:16, :].rearrange("p a n -> p (a n)").bitcast(F32)
            sqf = at[:, 1, 0:8, :].rearrange("p a n -> p (a n)").bitcast(F32)
            work = at[:, 1, 8:10, :].rearrange("p a n -> p (a n)").bitcast(F32)
            step = [0]

            def link(ins):
                step[0] += 1
                ins.then_inc(f_dve, 1)
                dve.wait_ge(f_dve, step[0])

            def by_graph(ap):
                return ap.rearrange("p (b c) -> p b c", c=C)

            def over_channels(ap):
                return ap.unsqueeze(2).broadcast_to([P, B, C])

            means, rest, about, other = [work[:, k * B * C:(k + 1) * B * C] for k in range(4)]
            dve.wait_ge(y_summed, B)
            dve.wait_ge(at_used, B * T + T)
            link(nc.vector.tensor_reduce(ht[:, 0:C], y_sum[:, :].rearrange("p (b c) -> p c b", c=C), AX.X, ALU.add))
            nc.vector.tensor_reduce(ht[:, C:C + 1], count[:, :], AX.X, ALU.add).then_inc(sums_ready, 1)
            link(nc.vector.tensor_tensor(by_graph(means), by_graph(y_sum[:, :]), over_channels(over[:, :]), ALU.mult))
            link(nc.vector.tensor_tensor(by_graph(other), by_graph(means), over_channels(count[:, :]), ALU.mult))
            link(nc.vector.tensor_tensor(rest, y_sum[:, :], other, ALU.subtract))
            one_over, mu, var = ht[:, 8 * C:8 * C + 1], ht[:, 6 * C:7 * C], ht[:, 3 * C:4 * C]
            dve.wait_ge(sums_mm, 1)
            link(nc.vector.reciprocal(one_over, acc[:, 0, C:C + 1]))
            link(nc.vector.tensor_scalar(mu, acc[:, 0, 0:C], one_over, None, ALU.mult))
            link(nc.vector.tensor_tensor(by_graph(about), by_graph(means), over_tiles(mu, B, C), ALU.subtract))
            link(nc.vector.tensor_tensor(by_graph(other), by_graph(about), over_channels(count[:, :]), ALU.mult))
            link(nc.vector.scalar_tensor_tensor(other, rest, 2.0, other, ALU.mult, ALU.add))
            link(nc.vector.tensor_tensor(other, other, about, ALU.mult))
            y_squares(B - 1)
            dve.wait_ge(y_stats, B)
            link(nc.vector.tensor_tensor(other, other, y_sqs[:, :], ALU.add))
            nc.vector.tensor_reduce(ht[:, 2 * C:3 * C], other.rearrange("p (b c) -> p c b", c=C), AX.X, ALU.add)\
              .then_inc(sums_ready, 1)
            dve.wait_ge(sums_mm, 2)
            link(nc.vector.tensor_scalar(var, acc[:, 1, 0:C], one_over, BN_EPS, ALU.mult, ALU.add))
            nc.vector.reciprocal(var, var).then_inc(var_inverse, 1)
            root, newton = ht[:, 4 * C:5 * C], ht[:, 5 * C:6 * C]
            dve.wait_ge(var_root, 1)
            link(nc.vector.reciprocal(newton, root))
            link(nc.vector.tensor_tensor(newton, newton, var, ALU.mult))
            link(nc.vector.tensor_tensor(root, root, newton, ALU.add))
            scale, shift = ht[:, 4 * C:5 * C], ht[:, 7 * C:8 * C]
            link(nc.vector.scalar_tensor_tensor(scale, root, 0.5, cbias[:, 3, :], ALU.mult, ALU.mult))
            link(nc.vector.tensor_tensor(shift, mu, scale, ALU.mult))
            nc.vector.tensor_tensor(shift, cbias[:, 4, :], shift, ALU.subtract).then_inc(shift_ready, 1)

            def graph(ap, b):
                return ap[:, b * NC_:(b + 1) * NC_]

            def graph_tiles(ap, b):
                return graph(ap, b).rearrange("p (t c) -> p t c", c=C)

            def z_scale(b):
                dve.wait_ge(fy_in[b], 16)
                nc.vector.tensor_tensor(graph_tiles(yf, b), graph_tiles(yf, b), over_tiles(scale, T, C), ALU.mult)\
                  .then_inc(z_scaled, 1)

            def z_residual(b):
                m = ht[:, MEANS + b % 2 * T:MEANS + (b % 2 + 1) * T]
                dve.wait_ge(fx_in[b], 16)
                dve.wait_ge(z_masked, b + 1)
                nc.vector.scalar_tensor_tensor(graph(xf, b), graph(yf, b), 0.0, graph(xf, b), ALU.max, ALU.add)\
                  .then_inc(z_step, 1)
                dve.wait_ge(z_step, 2 * b + 1)
                nc.vector.tensor_reduce(m, graph_tiles(xf, b), AX.X, ALU.add).then_inc(z_step, 1)
                dve.wait_ge(z_step, 2 * b + 2)
                nc.vector.tensor_scalar(m, m, -1.0 / C, None, ALU.mult).then_inc(z_mean, 1)

            def z_deviation(b):
                r = ht[:, INVERSE + b % 2 * T:INVERSE + (b % 2 + 1) * T]
                dve.wait_ge(z_sq, b + 1)
                nc.vector.tensor_reduce(r, graph_tiles(sqf, b), AX.X, ALU.add).then_inc(z_var, 1)
                dve.wait_ge(z_var, 2 * b + 1)
                nc.vector.tensor_scalar(r, r, 1.0 / C, LN_EPS, ALU.mult, ALU.add).then_inc(z_var, 1)
                dve.wait_ge(z_var, 2 * b + 2)
                nc.vector.reciprocal(r, r).then_inc(z_inverse, 1)

            def z_finish(b):
                w = b % 2 * T
                r, root, newton = [ht[:, k + w:k + w + T] for k in (INVERSE, ROOT, NEWTON)]
                dve.wait_ge(z_root, b + 1)
                nc.vector.reciprocal(newton, root).then_inc(z_newton, 1)
                dve.wait_ge(z_newton, 3 * b + 1)
                nc.vector.tensor_tensor(newton, newton, r, ALU.mult).then_inc(z_newton, 1)
                dve.wait_ge(z_newton, 3 * b + 2)
                nc.vector.tensor_tensor(root, root, newton, ALU.add).then_inc(z_newton, 1)
                dve.wait_ge(z_newton, 3 * b + 3)
                nc.vector.scalar_tensor_tensor(graph_tiles(xf, b), graph_tiles(xf, b), 0.5,
                                               root.unsqueeze(2).broadcast_to([P, T, C]), ALU.mult, ALU.mult)\
                  .then_inc(z_out, 1)

            z_scale(0)
            z_scale(1)
            for b in range(B + 2):
                if b < B:
                    z_residual(b)
                if b + 2 < B:
                    z_scale(b + 2)
                if 1 <= b <= B:
                    z_deviation(b - 1)
                if b >= 2:
                    z_finish(b - 2)

        @block.gpsimd
        def _(pool):
            def k_even(n, s, q):
                pool.wait_ge(row_used[q], n + 1 + OPEN)
                pool.wait_ge(gated[q], n + 1 + OPEN)
                k = k_slot[:, s, q * W:(q + 1) * W]
                nc.gpsimd.tensor_tensor(k, k, gate[:, 0, :], ALU.mult).then_inc(k_done[q], 1)

            start_at_one(pool, k_done[0], k_done[2])
            pool.wait_ge(u_step, 2)
            def scaled(b, jj, s):
                n = b * T + jj * 2 + s
                di = d[:, bass.ds(jj * 2 + s, 1)]
                pool.wait_ge(deg_done, n + 1)
                nc.gpsimd.tensor_tensor(di, deg[:, s, 1:2], half_neg[:, 0:1], ALU.pow).then_inc(d_done, 1)
                pool.wait_ge(d_done, n + 1)
                pool.wait_ge(x_in_done, (b + 1) * 16)
                pool.wait_ge(k_used[3], n - 1 + OPEN_K)
                nc.gpsimd.tensor_tensor(v[:, s, :], x[:, bass.ds((jj * 2 + s) * C, C)],
                                        di.broadcast_to([P, C]), ALU.mult).then_inc(v_done, 1)

            def stripe(b, jj, s, start=False):
                n = b * T + jj * 2 + s
                k_even(n, s, 0)
                if not start:
                    scaled(b, jj - 1 + s, 1 - s)
                k_even(n, s, 2)

            def residual(b, e):
                pool.wait_ge(x_lo, b * 6 + 2 * e + OPEN)
                all_x = x[:, :].rearrange("p (t c) -> p t c", c=C)
                bias_e = over_tiles(cbias[:, e - 1, :], T, C)
                if e == 1:
                    nc.gpsimd.tensor_tensor(sq_tiles, bias_e, spread_mask(b), ALU.mult).then_inc(res_step, 1)
                    pool.wait_ge(res_step, b + 1)
                    nc.gpsimd.tensor_tensor(x[:, :], x[:, :], sq, ALU.add).then_inc(res_done, 1)
                    pool.wait_ge(res_done, b * 2 + 1)
                else:
                    nc.gpsimd.tensor_tensor(all_x, all_x, bias_e, ALU.add).then_inc(res_done, 1)

            def spread_mask(b):
                return mask[:, bass.ds(b * T, T)].unsqueeze(2).broadcast_to([P, T, C])

            sq_tiles = sq.rearrange("p (t c) -> p t c", c=C)
            y_tiles = y[:, :].rearrange("p (t c) -> p t c", c=C)

            def stats(b):
                pool.wait_ge(y_done, b * 2 + 2)
                nc.gpsimd.tensor_tensor(sq_tiles, y_tiles, spread_mask(b), ALU.mult).then_inc(y_masked, 1)
                pool.wait_ge(y_shift, b + 1)
                nc.gpsimd.tensor_tensor(sq_tiles, y_tiles, over_tiles(y_mean, T, C), ALU.add).then_inc(y_diff, 1)

            def layers_0_to_2(b, with_stats=False):
                with pool.Fori(2, TP) as jj:
                    for s in range(2):
                        stripe(b, jj, s)
                scaled(b, TP - 1, 1)
                if type(b) is int and b == 0:
                    pool.wait_ge(u_step, U_STEPS)
                residual(b, 1)
                if with_stats:
                    stats(b - 1)
                residual(b, 2)

            def layer_3(b, more):
                if more:
                    for s in range(2):
                        stripe(b + 1, 0, s, start=(s == 0))
                    stripe(b + 1, 1, 0)
                for h in range(2):
                    r = slice(h * HALF, (h + 1) * HALF)
                    pool.wait_ge(y_floor, b * 2 + h + 1)
                    nc.gpsimd.tensor_tensor(rstd[:, 1, r], rstd[:, 0, r], half_neg[:, :], ALU.pow).then_inc(y_rstd, 1)
                if more:
                    stripe(b + 1, 1, 1)

            for jj in range(2):
                for s in range(2):
                    stripe(0, jj, s, start=(jj + s == 0))
            layers_0_to_2(0)
            with pool.Fori(1, B) as b:
                layer_3(b - 1, True)
                layers_0_to_2(b, True)
            layer_3(B - 1, False)
            stats(B - 1)

            yf = at[:, 0, 0:8, :].rearrange("p a n -> p (a n)").bitcast(F32)
            xf = at[:, 0, 8:16, :].rearrange("p a n -> p (a n)").bitcast(F32)
            pool.wait_ge(shift_ready, 1)
            for b in range(B + 1):
                if b < B:
                    z = yf[:, b * NC_:(b + 1) * NC_].rearrange("p (t c) -> p t c", c=C)
                    pool.wait_ge(z_scaled, b + 1)
                    nc.gpsimd.tensor_tensor(z, z, over_tiles(ht[:, 7 * C:8 * C], T, C), ALU.add).then_inc(z_shifted, 1)
                    pool.wait_ge(z_shifted, b + 1)
                    nc.gpsimd.tensor_tensor(z, z, spread_mask(b), ALU.mult).then_inc(z_masked, 1)
                if b >= 1:
                    r = xf[:, (b - 1) * NC_:b * NC_].rearrange("p (t c) -> p t c", c=C)
                    m = ht[:, MEANS + (b - 1) % 2 * T:MEANS + ((b - 1) % 2 + 1) * T]
                    pool.wait_ge(z_mean, b)
                    nc.gpsimd.tensor_tensor(r, r, m.unsqueeze(2).broadcast_to([P, T, C]), ALU.add).then_inc(z_centred, 1)


def kernel(x, adj, nodemask, L0_gnn_U, L0_gnn_w_scale, L1_gnn_W0, L1_gnn_b0, L1_gnn_W1, L1_gnn_b1, L1_gnn_W2,
           L1_gnn_b2, L1_gnn_Wout, L1_gnn_bout, L2_gnn_weight, L2_gnn_bias, L3_gnn_weight, L3_gnn_bias,
           L3_gnn_gamma, L3_gnn_beta):
    import numpy as np
    import concourse.bacc as bacc
    from concourse.bass_utils import run_bass_kernel_spmd

    products = [(0, 0), (0, 1), (1, 0), (1, 1), (0, 2), (2, 0), (1, 2), (2, 1)]
    pick = np.zeros((P, 4), np.float32)
    for g, sides in enumerate(products):
        for side, part in enumerate(sides):
            pick[g * R:(g + 1) * R, 2 * side] = -1.0 if part >= 1 else 0.0
            pick[g * R:(g + 1) * R, 2 * side + 1] = -1.0 if part >= 2 else 0.0
    eye = np.eye(P, dtype=np.float32)
    fold = np.eye(C, dtype=np.float32) - np.float32(1.0 / C)

    def a(v):
        return np.ascontiguousarray(np.asarray(v))

    arrays = {
        "x_in": a(np.asarray(x).reshape(B, T, P, C).transpose(0, 2, 1, 3)).reshape(B, P, NC_),
        "adj": a(adj),
        "mask_in": a(np.asarray(nodemask).reshape(B, T, P).transpose(2, 0, 1)).reshape(P, B * T),
        "ut": a(np.asarray(L0_gnn_U).T),
        "wscale": a(L0_gnn_w_scale).reshape(1),
        "w0": a(L1_gnn_W0), "w1": a(L1_gnn_W1), "w2": a(L1_gnn_W2), "wout": a(L1_gnn_Wout),
        "l2w": a(L2_gnn_weight), "l3w": a(L3_gnn_weight),
        "b0": a(L1_gnn_b0), "b1": a(L1_gnn_b1), "b2": a(L1_gnn_b2), "bout": a(L1_gnn_bout),
        "l2b": a(L2_gnn_bias), "l3b": a(L3_gnn_bias), "gamma": a(L3_gnn_gamma), "beta": a(L3_gnn_beta),
        "ident_in": eye, "fold_in": fold, "pick_in": pick,
    }
    nc = bacc.Bacc("TRN2", target_bir_lowering=False, num_devices=1)
    args = {n: nc.dram_tensor(n, v.shape, mybir.dt.from_np(v.dtype), kind="ExternalInput").ap()
            for n, v in arrays.items()}
    out = nc.dram_tensor("out", (B, P, NC_), F32, kind="ExternalOutput").ap()
    build(nc, *args.values(), out)
    r = run_bass_kernel_spmd(nc, [arrays], core_ids=[0])
    got = r.results[0]["out"]
    return got.reshape(B, P, T, C).transpose(0, 2, 1, 3).reshape(B, N, C)
```
